# Optimizing a Trainium2 kernel written in Bass

```python
import numpy as np
import jax
import jax.numpy as jnp

def _softmax(x, axis=-1):
    return jax.nn.softmax(x, axis=axis)

def _gelu(x):
    return jax.nn.gelu(x, approximate=True)

def _silu(x):
    return jax.nn.silu(x)

def _sigmoid(x):
    return jax.nn.sigmoid(x)

def _layernorm(x, axis=-1, eps=1e-05):
    m = jnp.mean(x, axis=axis, keepdims=True)
    v = jnp.var(x, axis=axis, keepdims=True)
    return (x - m) / jnp.sqrt(v + eps)

def _scatter_add(tgt, idx, src, axis=0):
    return tgt.at[idx].add(src)

def _segment_sum(src, seg, n):
    return jax.ops.segment_sum(src, seg, n)
kernel_name = 'mk_gnn_resnorm_d2_gnn_r16_c739b2'

def setup_inputs(seed: int=0):
    np.random.seed(seed)
    _w = jnp.asarray

    def _rec_inputs():
        import jax
        import jax.numpy as jnp
        _gk = jax.random.key(seed)
        x = -0.0006008 + 1.001 * jax.random.normal(jax.random.fold_in(_gk, 1), (6250, 256), jnp.float32)
        src = jax.random.randint(jax.random.fold_in(_gk, 2), (100000,), 0, 6250, jnp.int32)
        dst = jnp.minimum((6250 * jax.random.uniform(jax.random.fold_in(_gk, 3), (100000,)) ** 2.0).astype(jnp.int32), 99999)
        _o = jnp.argsort(dst, stable=True)
        src = src[_o]
        dst = dst[_o]
        edge_attr_64 = 0.000312547 + 1.00004 * jax.random.normal(jax.random.fold_in(_gk, 11), (100000, 64), jnp.float32)
        return (x, src, dst, edge_attr_64)
    x, src, dst, edge_attr_64 = _rec_inputs()

    def _L0_gnn_setup():
        import jax, jax.numpy as jnp
        import numpy as np
        N, E, H, DE = (625, 15625, 256, 64)
        EPS = 1e-05

        def _lin_init(k, fan_in, shape):
            s = 1.0 / np.sqrt(fan_in)
            return jax.random.uniform(k, shape, jnp.float32, -s, s)
        key = jax.random.key(seed)
        ks = jax.random.split(key, 12)
        x = jax.random.normal(ks[0], (N, H), jnp.float32)
        edge_index = jax.random.randint(ks[1], (2, E), 0, N)
        edge_attr = jax.random.normal(ks[2], (E, DE), jnp.float32)
        d_in = H + DE
        W1 = _lin_init(ks[3], d_in, (d_in, H))
        b1 = _lin_init(ks[4], d_in, (H,))
        W2 = _lin_init(ks[5], H, (H, H))
        b2 = _lin_init(ks[6], H, (H,))
        Wg = _lin_init(ks[7], d_in, (d_in, H))
        bg = _lin_init(ks[8], d_in, (H,))
        gamma = jnp.ones((H,), jnp.float32)
        beta = jnp.zeros((H,), jnp.float32)
        return {'x': x, 'edge_index': edge_index, 'edge_attr': edge_attr, 'W1': W1, 'b1': b1, 'W2': W2, 'b2': b2, 'Wg': Wg, 'bg': bg, 'gamma': gamma, 'beta': beta}
    _L0_gnn_all = _L0_gnn_setup()
    _L0_gnn_in = {k: v for k, v in _L0_gnn_all.items() if k in ('W1', 'b1', 'W2', 'b2', 'Wg', 'bg', 'gamma', 'beta')}
    del _L0_gnn_all

    def _L1_gnn_setup():
        import jax, jax.numpy as jnp
        import numpy as np
        N_NODES = 3125
        N_EDGES = 50000
        N_FEAT = 256
        N_CLASSES = 256
        K_HOPS = 2
        key = jax.random.key(seed)
        k1, k2, k3 = jax.random.split(key, 3)
        x = jax.random.normal(k1, (N_NODES, N_FEAT), dtype=jnp.float32)
        edge_index = jax.random.randint(k2, (2, N_EDGES), 0, N_NODES, dtype=jnp.int32)
        W = jax.random.normal(k3, (N_CLASSES, N_FEAT), dtype=jnp.float32) * 0.05
        b = jnp.zeros((N_CLASSES,), dtype=jnp.float32)
        return {'x': x, 'edge_index': edge_index, 'W': W, 'b': b}
    _L1_gnn_all = _L1_gnn_setup()
    _L1_gnn_in = {k: v for k, v in _L1_gnn_all.items() if k in ('W', 'b')}
    del _L1_gnn_all
    return {'x': x, 'src': src, 'dst': dst, 'edge_attr_64': edge_attr_64, 'L0_gnn_W1': _L0_gnn_in['W1'], 'L0_gnn_b1': _L0_gnn_in['b1'], 'L0_gnn_W2': _L0_gnn_in['W2'], 'L0_gnn_b2': _L0_gnn_in['b2'], 'L0_gnn_Wg': _L0_gnn_in['Wg'], 'L0_gnn_bg': _L0_gnn_in['bg'], 'L0_gnn_gamma': _L0_gnn_in['gamma'], 'L0_gnn_beta': _L0_gnn_in['beta'], 'L1_gnn_W': _L1_gnn_in['W'], 'L1_gnn_b': _L1_gnn_in['b']}

def reference(x, src, dst, edge_attr_64, L0_gnn_W1, L0_gnn_b1, L0_gnn_W2, L0_gnn_b2, L0_gnn_Wg, L0_gnn_bg, L0_gnn_gamma, L0_gnn_beta, L1_gnn_W, L1_gnn_b):
    import jax
    import jax.numpy as jnp

    def _L0_gnn_ref(x, edge_index, edge_attr, W1, b1, W2, b2, Wg, bg, gamma, beta):
        import jax, jax.numpy as jnp
        import numpy as np
        N, E, H, DE = (625, 15625, 256, 64)
        EPS = 1e-05

        def _lin_init(k, fan_in, shape):
            s = 1.0 / np.sqrt(fan_in)
            return jax.random.uniform(k, shape, jnp.float32, -s, s)
        src, dst = (edge_index[0], edge_index[1])
        ei = jnp.concatenate([x[src], edge_attr], axis=-1)
        core = jnp.maximum(ei @ W1 + b1, 0.0) @ W2 + b2
        gate = jax.nn.sigmoid(ei @ Wg + bg)
        msg = gate * core
        agg = jax.ops.segment_sum(msg, dst, num_segments=x.shape[0])
        out = agg + x
        mu = jnp.mean(out, axis=-1, keepdims=True)
        var = jnp.var(out, axis=-1, keepdims=True)
        out = (out - mu) * jax.lax.rsqrt(var + EPS) * gamma + beta
        return out

    def _L1_gnn_ref(x, edge_index, W, b):
        import jax, jax.numpy as jnp
        import numpy as np
        N_NODES = 3125
        N_EDGES = 50000
        N_FEAT = 256
        N_CLASSES = 256
        K_HOPS = 2
        n = x.shape[0]
        loop = jnp.arange(n, dtype=edge_index.dtype)
        row = jnp.concatenate([edge_index[0], loop])
        col = jnp.concatenate([edge_index[1], loop])
        deg = jax.ops.segment_sum(jnp.ones_like(col, dtype=x.dtype), col, num_segments=n)
        dinv = jnp.where(deg > 0, jax.lax.rsqrt(deg), jnp.zeros_like(deg))
        norm = dinv[row] * dinv[col]

        def hop(h, _):
            msg = h[row] * norm[:, None]
            h_new = jax.ops.segment_sum(msg, col, num_segments=n)
            return (h_new, None)
        h, _ = jax.lax.scan(hop, x, None, length=K_HOPS)
        logits = h @ W.T + b
        return jax.nn.log_softmax(logits, axis=1)
    edge_index = jnp.stack([src, dst])
    x = _layernorm(x + _L0_gnn_ref(x, edge_index, edge_attr_64, L0_gnn_W1, L0_gnn_b1, L0_gnn_W2, L0_gnn_b2, L0_gnn_Wg, L0_gnn_bg, L0_gnn_gamma, L0_gnn_beta), axis=-1)
    x = _layernorm(x + _L1_gnn_ref(x, edge_index, L1_gnn_W, L1_gnn_b), axis=-1)
    return x

_drawn_inputs = setup_inputs


def setup_inputs(seed=0):
    import zlib

    import numpy as np

    out = dict(_drawn_inputs(seed))
    spreads = {'L0_gnn_gamma': (1.0, 0.2), 'L0_gnn_beta': (0.0, 0.1), 'L1_gnn_b': (0.0, 0.1)}
    factors = {'L0_gnn_bg': 8.0}
    for name, (base, spread) in spreads.items():
        noise = np.random.default_rng([zlib.crc32(name.encode()), seed]).standard_normal(out[name].shape)
        drawn = base * np.exp(spread * noise) if base else spread * noise
        out[name] = jnp.asarray(drawn.astype(out[name].dtype))
    for name, factor in factors.items():
        out[name] = (out[name] * factor).astype(out[name].dtype)
    return out
```

```python
from contextlib import ExitStack

import numpy as np

import concourse.bass as bass
import concourse.mybir as mybir

P = 128
GROUP = 512
TILES = 4
WINDOW = 128
NODES = 125
STEP = 2 * TILES
EPS = 1e-5

F32 = mybir.dt.float32
F32R = mybir.dt.float32r
BF16 = mybir.dt.bfloat16
I32 = mybir.dt.int32
ALU = mybir.AluOpType
ACT = mybir.ActivationFunctionType
AX = mybir.AxisListType
ds = bass.ds


def wait_count(engine, semaphore, count):
    if not isinstance(count, int) or count > 0:
        engine.wait_ge(semaphore, count)


def over_tiles(engine, step, first, last, turns):
    for t in range(first, STEP):
        step(t // STEP, t % STEP)
    with engine.Fori(1, turns - 1) as i:
        for u in range(STEP):
            step(i, u)
    for t in range(STEP * (turns - 1), last):
        step(t // STEP, t % STEP)


def ahead(i, u, lag):
    turn, place = i + (u + lag) // STEP, (u + lag) % STEP
    return turn, place, STEP * turn + place


def gnn_kernel(nc, x, src, dst, edge_attr, W1, b1, W2, b2, Wg, bg, gamma, beta, Wl, bl, out):
    N, H = x.shape
    E, DE = edge_attr.shape
    KC = H // P
    H2 = 2 * H
    NG = -(-E // GROUP)
    R = NG // 2
    NT = NG * TILES
    OVERLAP = NG * GROUP - E
    NN = N // NODES
    NB = -(-N // WINDOW)
    NCOL = N + WINDOW
    assert KC * P == H and 2 * DE == P and NG % 2 == 0 and R <= P and OVERLAP < GROUP
    assert NN * NODES == N and NN % 2 == 0 and NB <= P and H2 == 512 and R > 2

    p_table = nc.dram_tensor("p_table", (N, H2), F32, kind="Internal").ap()
    hop_table = [nc.dram_tensor(f"hop_table{k}", (N, H), F32, kind="Internal").ap() for k in range(2)]
    dinv_flat = nc.dram_tensor("dinv_flat", (NB * P,), F32, kind="Internal").ap()

    with ExitStack() as ctx:
        def sb(name, shape, dt=F32):
            return ctx.enter_context(nc.sbuf_tensor(name, shape, dt))

        def sem(name):
            return ctx.enter_context(nc.semaphore(name))

        banks = ctx.enter_context(nc.psum_tensor("banks", [P, 8, 512], F32))

        w_e_hi = sb("w_e_hi", [P, H2], F32R)
        w_e_lo = sb("w_e_lo", [P, H2], F32R)
        w_2 = sb("w_2", [P, KC, H])
        w_l_turned = sb("w_l_turned", [P, KC, H])
        bias_in = sb("bias_in", [P, H2])
        bias_core = sb("bias_core", [P, H])
        gamma_all = sb("gamma_all", [P, H])
        beta_all = sb("beta_all", [P, H])
        bias_l = sb("bias_l", [P, H])
        ident = sb("ident", [P, P])
        iota = sb("iota", [P, P])
        iota_b = sb("iota_b", [P, P], BF16)
        block_starts = sb("block_starts", [P, NB])

        pair = 2 * GROUP
        x3_room = sb("x3_room", [P, max(NN * H, 9 * pair)])
        x3 = x3_room[0:NODES, 0:NN * H].rearrange("p (t n) -> p t n", n=H)

        def rows_at(k, dt):
            return x3_room[:, k * pair:(k + 1) * pair].bitcast(dt).rearrange("p (s e) -> p s e", s=2)

        index_rows = x3_room[:, 0:4 * pair].rearrange("p (k s e) -> p k s e", k=4, s=2)
        dst_f = rows_at(4, F32)
        dst_rows, src_rows, hi_i, lo_i = (rows_at(k, I32) for k in range(5, 9))
        base_f = sb("base_f", [P, 2])
        top_f = sb("top_f", [P, 2])
        span_f = sb("span_f", [P, 2])
        span_max = sb("span_max", [P, 1])
        widest = sb("widest", [1, 1])
        fits = sb("fits", [1, 1], I32)
        bases = sb("bases", [2, R], I32)
        src_t = sb("src_t", [P, NT], I32)
        local_t = sb("local_t", [P, NT])
        hi_t = sb("hi_t", [P, NT])
        lo_t = sb("lo_t", [P, NT])

        agg = sb("agg", [P, KC, NCOL])
        dinv_all = sb("dinv_all", [P, N])
        dinv_col = sb("dinv_col", [NODES, NN])
        dinv_rows = sb("dinv_rows", [NB, P])

        hot = sb("hot", [P, STEP, WINDOW])
        gathered = sb("gathered", [P, 2, TILES, H2])
        start_room = gathered[:, :, :, :].rearrange("p s j n -> p (s j n)")
        w_e = start_room[:, 0:H2]
        w_l = start_room[:, H2:H2 + KC * H].rearrange("p (k n) -> p k n", k=KC)
        iota_i = start_room[:, 2 * H2:2 * H2 + P].bitcast(I32)
        block_i = start_room[:, 3 * H2:3 * H2 + NB].bitcast(I32)
        index_now = sb("index_now", [P, 2, TILES], I32)
        ea = sb("ea", [P, 2, TILES, DE])
        ea_parts = sb("ea_parts", [P, TILES, 2, DE], F32R)
        ea_turned_sb = sb("ea_turned_sb", [P, 2, GROUP], F32R)
        pre_room = sb("pre_room", [P, 2 * H2])
        pre = pre_room[:, :].rearrange("p (h n) -> p h n", h=2)
        hot_lo = pre_room[:, 0:STEP * P // 2].bitcast(BF16).rearrange("p (u n) -> p u n", u=STEP)
        hot_hi = pre_room[:, STEP * P // 2:STEP * P // 2 + STEP * NB // 2].bitcast(BF16).rearrange("p (u n) -> p u n", u=STEP)
        hidden = sb("hidden", [P, 2, KC, P])
        gate = sb("gate", [P, 2, H])
        core = sb("core", [P, H])
        room = sb("room", [P, STEP * H])
        w_x = room[:, 0:KC * H2].rearrange("p (k n) -> p k n", k=KC)
        p_t = room[0:NODES, KC * H2:KC * H2 + 2 * H2].rearrange("p (h n) -> p h n", h=2)
        msg = room[:, :].rearrange("p (u n) -> p u n", u=STEP)
        node, xb_t, g_t = (room[0:NODES, k * 2 * H:(k + 1) * 2 * H].rearrange("p (h n) -> p h n", h=2)
                           for k in range(3))
        y_t = xb_t
        expo = room[0:NODES, 6 * H:7 * H]
        x_t = sb("x_t", [NODES, 2, H])
        x_turned_sb = sb("x_turned_sb", [P, 2, KC, NODES])
        stats = sb("stats", [NODES, 2, 6])
        moments = sb("moments", [NODES, 3, NN, 2])
        moments_now = sb("moments_now", [NODES, 2, 2])
        rstd = sb("rstd", [NODES, 3, NN])
        top = sb("top", [NODES, 2, 2])
        sums = sb("sums", [NODES, 2])
        lse = sb("lse", [NODES, 2])

        names = """setup_loaded consts_ready iota_made rows_made tables_turned tables_copied w_turned
        w_copied w_split base_turned fits_known pool_masked self_dve
        xa_turned xa_ready p_product p_ready
        deg_hot deg_counted deg_made deg_rooted dinv_made dinv_stored dinv_loaded agg_cleared
        p_index ea_split ea_turned ea_ready edge_product pre_ready pre_turned hidden_ready gate_ready core_done
        core_biased msg_ready hot_ready scattered agg_added slow_hot slow_scattered slow_added
        win_copied win_turned node_summed first_normed first_scaled first_summed
        stats_ready moments_ready moments_kept gathers_begun slow_begun variances_ready deviations_ready rstd_ready
        ea_rounded dinv_squared xb_ready x3_ready g_ready g_turned g_back
        hop_scaled hop_turned hop_ready hop_back
        logits_done logit_rows logit_top l_chain expd logd log_softmax y_summed y_ready""".split()
        S = {n: sem(n) for n in names}
        for k in range(2):
            for n in "index hot_ready scattered agg_added slow_hot slow_scattered slow_added".split():
                S[f"h{k}_{n}"] = sem(f"h{k}_{n}")
            for n in ("p_gathered", "ea_loaded", "p_stored", "g_stored", "hop_stored", "y_stored", "xa_loaded", "xn_loaded", "xb_loaded", "h0_gathered", "h1_gathered"):
                S[f"{n}{k}"] = sem(f"{n}{k}")

        setup_dmas = [0]
        block = ctx.enter_context(nc.Block())

        def node_rows(table, t):
            return table[ds(NODES * t, NODES), :] if not isinstance(t, int) else table[NODES * t:NODES * (t + 1), :]

        def node_cols(table, t):
            return table[:, :, ds(NODES * t, NODES)] if not isinstance(t, int) else table[:, :, NODES * t:NODES * (t + 1)]

        @block.sync
        def _(sp):
            def load(to, of):
                sp.dma_start(to, of).then_inc(S["setup_loaded"], 16)
                setup_dmas[0] += 1

            full = (R - 1) * 2 * GROUP
            for rows, index in ((dst_rows, dst), (src_rows, src)):
                load(rows[0:R - 1, :, :], index[0:full].rearrange("(r s e) -> r s e", s=2, e=GROUP))
                load(rows[R - 1:R, 0, :], index[full:full + GROUP].rearrange("(r e) -> r e", r=1))
                load(rows[R - 1:R, 1, :], index[E - GROUP:E].rearrange("(r e) -> r e", r=1))
            for n, w in enumerate((W1, Wg)):
                cols = slice(n * H, (n + 1) * H)
                load(w_x[:, :, cols], w[0:H, :].rearrange("(k p) n -> p k n", p=P))
                load(w_e[0:DE, cols], w[H:H + DE, :])
                load(w_e[DE:P, cols], w[H:H + DE, :])
            load(bias_in[:, 0:H], b1.partition_broadcast(P))
            load(bias_in[:, H:H2], bg.partition_broadcast(P))
            load(w_2[:, :, :], W2.rearrange("(k p) n -> p k n", p=P))
            load(w_l[:, :, :], Wl.rearrange("(k p) n -> p k n", p=P))
            for to, of in ((bias_core, b2), (gamma_all, gamma), (beta_all, beta), (bias_l, bl)):
                load(to[:, :], of.partition_broadcast(P))

            def load_xa(i, h):
                t = 2 * i + h
                wait_count(sp, S["xa_turned"], t - 1)
                sp.dma_start(x_t[:, h, :], node_rows(x, t)).then_inc(S[f"xa_loaded{h}"], 16)

            for h in range(2):
                load_xa(0, h)
            with sp.Fori(1, NN // 2) as i:
                for h in range(2):
                    load_xa(i, h)

            sp.wait_ge(S["dinv_made"], 1)
            sp.dma_start(dinv_flat.rearrange("(b n) -> b n", n=P), dinv_rows[:, :]).then_inc(S["dinv_stored"], 16)
            sp.wait_ge(S["dinv_stored"], 16)
            with nc.allow_non_contiguous_dma("once, a few thousand words"):
                sp.dma_start(dinv_col[:, :], dinv_flat[0:N].rearrange("(t p) -> p t", p=NODES)).then_inc(
                    S["dinv_loaded"], 16)
            sp.dma_start(dinv_all[:, :], dinv_flat[0:N].partition_broadcast(P)).then_inc(S["dinv_loaded"], 16)

            def load_ea(i, s):
                g = 2 * i + s
                wait_count(sp, S["ea_split"], g - 1)
                if isinstance(g, int):
                    e0 = min(GROUP * g, E - GROUP)
                    rows = edge_attr[e0:e0 + GROUP, :]
                else:
                    rows = edge_attr[ds(GROUP * g, GROUP), :]
                sp.dma_start(ea[:, s, :, :], rows.rearrange("(p j) d -> p j d", j=TILES)).then_inc(
                    S[f"ea_loaded{s}"], 16)

            for s in range(2):
                load_ea(0, s)
            with sp.Fori(1, R - 1) as i:
                for s in range(2):
                    load_ea(i, s)
            for s in range(2):
                load_ea(R - 1, s)

            sp.wait_ge(S["xa_turned"], NN)

            def load_xn(i, h):
                t = 2 * i + h
                wait_count(sp, S["node_summed"], t - 1)
                sp.dma_start(x_t[:, h, :], node_rows(x, t)).then_inc(S[f"xn_loaded{h}"], 16)

            def load_xb(i, h):
                t = 2 * i + h
                wait_count(sp, S["xb_ready"], t - 1)
                sp.dma_start(x_t[:, h, :], node_rows(x, t)).then_inc(S[f"xb_loaded{h}"], 16)

            for load_x in (load_xn, load_xb):
                if load_x is load_xb:
                    sp.wait_ge(S["node_summed"], NN)
                for h in range(2):
                    load_x(0, h)
                with sp.Fori(1, NN // 2) as i:
                    for h in range(2):
                        load_x(i, h)

            def store_y(i, h):
                t = 2 * i + h
                sp.wait_ge(S["y_ready"], t + 1)
                sp.dma_start(node_rows(out, t), y_t[:, h, :]).then_inc(S[f"y_stored{h}"], 16)

            with sp.Fori(0, NN // 2) as i:
                for h in range(2):
                    store_y(i, h)
            for h in range(2):
                sp.wait_ge(S[f"y_stored{h}"], 8 * NN)

        @block.gpsimd
        def _(pool):
            nc.gpsimd.memset(ident[:, :], 0.0).then_inc(S["iota_made"], 1)
            nc.gpsimd.iota(iota_i[:, :], pattern=[[1, P]], base=0, channel_multiplier=0).then_inc(S["iota_made"], 1)
            nc.gpsimd.iota(block_i[:, :], pattern=[[-WINDOW, NB]], base=0, channel_multiplier=0).then_inc(
                S["iota_made"], 1)
            pool.wait_ge(S["iota_made"], 3)
            nc.gpsimd.affine_select(out=ident[:, :], in_=ident[:, :], compare_op=ALU.not_equal, fill=1.0, base=0,
                                    pattern=[[-1, P]], channel_multiplier=1).then_inc(S["consts_ready"], 1)
            nc.gpsimd.memset(agg[:, :, :], 0.0).then_inc(S["agg_cleared"], 1)

            pool.wait_ge(S["rows_made"], 1)
            if OVERLAP:
                for table in (1, 2):
                    rows = index_rows[0:R, table, 1, :]
                    nc.gpsimd.affine_select(
                        out=rows, in_=rows, compare_op=ALU.is_ge, fill=-1.0, base=(R - 1) * 2 * GROUP - OVERLAP,
                        pattern=[[1, GROUP]], channel_multiplier=-2 * GROUP).then_inc(S["pool_masked"], 1)

            def store_p(i, h):
                t = 2 * i + h
                pool.wait_ge(S["p_ready"], t + 1)
                pool.dma_start(node_rows(p_table, t), p_t[:, h, :]).then_inc(S[f"p_stored{h}"], 16)

            with pool.Fori(0, NN // 2) as i:
                for h in range(2):
                    store_p(i, h)
            def gather(table, width, stored, index, done, free, i, s):
                g = 2 * i + s
                wait_count(pool, S[free], TILES * (g - 1))
                if isinstance(g, int) and g == 0:
                    for h in range(2):
                        pool.wait_ge(S[f"{stored}{h}"], 8 * NN)
                pool.wait_ge(S[index], g + 1)
                pool.sem_inc(S["gathers_begun"], 1)
                for j in range(TILES):
                    pool.indirect_dma_start(
                        out=gathered[:, s, j, 0:width], out_offset=None, in_=table[:, :],
                        in_offset=bass.IndirectOffsetOnAxis(ap=index_now[:, s, j:j + 1], axis=0),
                    ).then_inc(S[f"{done}{s}"], 16)

            def gather_all(table, width, stored, index, done, free):
                for s in range(2):
                    gather(table, width, stored, index, done, free, 0, s)
                with pool.Fori(1, R) as i:
                    for s in range(2):
                        gather(table, width, stored, index, done, free, i, s)

            gather_all(p_table, H2, "p_stored", "p_index", "p_gathered", "pre_ready")

            def add_beta(i, h):
                t = 2 * i + h
                pool.wait_ge(S[f"xb_loaded{h}"], 16 * (i + 1))
                wait_count(pool, S["first_summed"], t - 1)
                nc.gpsimd.tensor_tensor(xb_t[:, h, :], x_t[:, h, :], beta_all[0:NODES, :], ALU.add).then_inc(
                    S["xb_ready"], 1)

            for h in range(2):
                add_beta(0, h)
            with pool.Fori(1, NN // 2) as i:
                for h in range(2):
                    add_beta(i, h)

            def store_g(i, h):
                t = 2 * i + h
                pool.wait_ge(S["g_ready"], t + 1)
                pool.dma_start(node_rows(hop_table[0], t), g_t[:, h, :]).then_inc(S[f"g_stored{h}"], 16)

            with pool.Fori(0, NN // 2) as i:
                for h in range(2):
                    store_g(i, h)

            gather_all(hop_table[0], H, "g_stored", "h0_index", "h0_gathered", "h0_scattered")

            def store_hop(i, h):
                t = 2 * i + h
                pool.wait_ge(S["hop_scaled"], t + 1)
                where = node_cols(agg, t)
                nc.gpsimd.tensor_copy(where, x_turned_sb[:, h, :, :]).then_inc(S["hop_back"], 1)
                pool.wait_ge(S["hop_ready"], t + 1)
                pool.dma_start(node_rows(hop_table[1], t), g_t[:, h, :]).then_inc(S[f"hop_stored{h}"], 16)

            with pool.Fori(0, NN // 2) as i:
                for h in range(2):
                    store_hop(i, h)
            for h in range(2):
                pool.wait_ge(S[f"hop_stored{h}"], 8 * NN)

            gather_all(hop_table[1], H, "hop_stored", "h1_index", "h1_gathered", "h1_scattered")

        @block.tensor
        def _(pe):
            pe.wait_ge(S["consts_ready"], 1)
            pe.wait_ge(S["setup_loaded"], 16 * setup_dmas[0])

            for o in range(KC):
                for k in range(KC):
                    at = (k * KC + o) * P
                    last = nc.tensor.transpose(banks[:, 5, at:at + P], w_l[:, o, k * P:(k + 1) * P], ident[:, :])
            last.then_inc(S["w_turned"], 1)

            pe.wait_ge(S["rows_made"], 1)
            if OVERLAP:
                pe.wait_ge(S["pool_masked"], 2)
            for table in range(4):
                wait_count(pe, S["tables_copied"], table)
                for s in range(2):
                    for j in range(TILES):
                        last = nc.tensor.transpose(banks[:, 6 + s, j * R:(j + 1) * R],
                                                   index_rows[0:R, table, s, j:GROUP:TILES], ident[0:R, 0:R])
                last.then_inc(S["tables_turned"], 1)
            nc.tensor.transpose(banks[0:2, 4, 0:R], base_f[0:R, :], ident[0:R, 0:R])
            nc.tensor.transpose(banks[0:1, 4, P:P + R], span_max[0:R, :], ident[0:R, 0:R]).then_inc(S["base_turned"], 1)

            def turn_x(i, h):
                t = 2 * i + h
                pe.wait_ge(S[f"xa_loaded{h}"], 16 * (i + 1))
                wait_count(pe, S["xa_ready"], t - 1)
                for k in range(KC):
                    last = nc.tensor.transpose(banks[:, h, k * NODES:(k + 1) * NODES],
                                               x_t[:, h, k * P:(k + 1) * P], ident[0:NODES, 0:NODES])
                last.then_inc(S["xa_turned"], 1)

            def product_x(i, h):
                t = 2 * i + h
                pe.wait_ge(S["xa_ready"], t + 1)
                wait_count(pe, S["p_ready"], t - 1)
                for k in range(KC):
                    last = nc.tensor.matmul(banks[0:NODES, 2 + h, :], x_turned_sb[:, h, k, :], w_x[:, k, :],
                                            start=k == 0, stop=k == KC - 1)
                last.then_inc(S["p_product"], 1)

            turn_x(0, 0)
            turn_x(0, 1)
            for h in range(2):
                product_x(0, h)
                turn_x(1, h)
            with pe.Fori(2, NN // 2) as i:
                for h in range(2):
                    product_x(i - 1, h)
                    turn_x(i, h)
            for h in range(2):
                product_x(NN // 2 - 1, h)

            def count(i, u):
                t = STEP * i + u
                pe.wait_ge(S["deg_hot"], t + 1)
                nc.tensor.matmul(banks[0:NB, 4, 0:P], hot_hi[:, u, :], hot_lo[:, u, :],
                                 start=isinstance(t, int) and t == 0, stop=isinstance(t, int) and t == NT - 1,
                                 skip_group_check=True).then_inc(S["deg_counted"], 1)

            pe.wait_ge(S["fits_known"], 1)
            over_tiles(pe, count, 0, NT, R)

            pe.wait_ge(S["xa_ready"], NN)
            pe.wait_ge(S["p_ready"], NN)
            pe.wait_ge(S["dinv_made"], 1)
            pe.wait_ge(S["w_copied"], 1)
            pe.wait_ge(S["tables_copied"], 4)
            pe.wait_ge(S["w_split"], 1)

            def turn_ea(turn, s):
                g = 2 * turn + s
                if isinstance(g, int) and not 0 <= g < NG:
                    return
                pe.wait_ge(S["ea_split"], g + 1)
                wait_count(pe, S["ea_ready"], g)
                for j in range(TILES):
                    last = nc.tensor.transpose(banks[:, 7, j * P:(j + 1) * P],
                                               ea_parts[:, j, :, :].rearrange("p a d -> p (a d)").bitcast(F32),
                                               ident[:, :])
                last.then_inc(S["ea_turned"], 1)

            def edge_product(turn, u, t):
                if isinstance(t, int) and not 0 <= t < NT:
                    return
                s, j = u // TILES, u % TILES
                if j == 0:
                    pe.wait_ge(S["ea_ready"], 2 * turn + s + 1)
                wait_count(pe, S["pre_ready"], t - 1)
                lhs = ea_turned_sb[:, s, j * P:(j + 1) * P]
                nc.tensor.matmul(banks[:, u % 2, :], lhs, w_e_hi[:, :], start=True, stop=False)
                nc.tensor.matmul(banks[:, u % 2, :], lhs, w_e_lo[:, :], start=False, stop=True).then_inc(
                    S["edge_product"], 1)

            def turn_pre(turn, u, t):
                if isinstance(t, int) and not 0 <= t < NT:
                    return
                pe.wait_ge(S["pre_ready"], t + 1)
                wait_count(pe, S["hidden_ready"], t - 1)
                for k in range(KC):
                    last = nc.tensor.transpose(banks[:, 2 + u % 2, k * P:(k + 1) * P],
                                               pre[:, u % 2, k * P:(k + 1) * P], ident[:, :])
                last.then_inc(S["pre_turned"], 1)

            def core_product(turn, u, t):
                if isinstance(t, int) and not 0 <= t < NT:
                    return
                pe.wait_ge(S["hidden_ready"], t + 1)
                wait_count(pe, S["msg_ready"], t - 1)
                for k in range(KC):
                    last = nc.tensor.matmul(banks[:, 4 + u % 2, 0:H], hidden[:, u % 2, k, :], w_2[:, k, :],
                                            start=k == 0, stop=k == KC - 1)
                last.then_inc(S["core_done"], 1)

            def scatter(rows_of, ready, hop, turn, u, t):
                if isinstance(t, int) and not 0 <= t < NT:
                    return
                s, j = u // TILES, u % TILES
                ready(turn, u, t)
                pe.wait_ge(S[hop + "hot_ready"], t + 1)
                if j == 0:
                    wait_count(pe, S[hop + "agg_added"], 2 * turn + s)
                for k in range(KC):
                    last = nc.tensor.matmul(banks[:, 6, k * WINDOW:(k + 1) * WINDOW],
                                            rows_of(u)[:, k * P:(k + 1) * P], hot[:, u, :],
                                            start=j == 0 and k == 0, stop=j == TILES - 1, skip_group_check=True)
                last.then_inc(S[hop + "scattered"], 1)

            def scatter_anywhere(rows_of, ready, hop, turn, u, t):
                if isinstance(t, int) and not 0 <= t < NT:
                    return
                s, j = u // TILES, u % TILES
                ready(turn, u, t)
                if j < TILES - 1:
                    return
                g = 2 * turn + s
                pe.sem_inc(S["slow_begun"], 1)
                with pe.Fori(0, NB) as w:
                    pe.wait_ge(S[hop + "slow_hot"], g * NB + w + 1)
                    pe.wait_ge(S[hop + "slow_added"], g * NB + w + 1)
                    for jj in range(TILES):
                        uu = TILES * s + jj
                        for k in range(KC):
                            last = nc.tensor.matmul(banks[:, 6, k * WINDOW:(k + 1) * WINDOW],
                                                    rows_of(uu)[:, k * P:(k + 1) * P], hot[:, uu, :],
                                                    start=jj == 0 and k == 0, stop=jj == TILES - 1,
                                                    skip_group_check=True)
                    last.then_inc(S[hop + "slow_scattered"], 1)

                pe.wait_ge(S[hop + "slow_added"], (g + 1) * NB + 1)
                for _ in range(TILES):
                    pe.sem_inc(S[hop + "scattered"], 1)

            def msg_of(u):
                return msg[:, u, :]

            def msg_is_ready(turn, u, t):
                pe.wait_ge(S["msg_ready"], t + 1)

            def edge_steps(scatter_stage):
                def step(i, u):
                    edge_product(*ahead(i, u, 2))
                    turn_pre(*ahead(i, u, 1))
                    core_product(*ahead(i, u, 0))
                    scatter_stage(msg_of, msg_is_ready, "", *ahead(i, u, -1))
                    if u % TILES == 0:
                        turn, place, _ = ahead(i, u, TILES)
                        turn_ea(turn, place // TILES)
                over_tiles(pe, step, -TILES, NT + 1, R)

            in_order = pe.value_load(fits[0:1, 0:1], min_val=0, max_val=1)
            with pe.If(in_order):
                edge_steps(scatter)
            with pe.Else():
                edge_steps(scatter_anywhere)

            def turn_win(t, h):
                pe.wait_ge(S["win_copied"], t + 1)
                wait_count(pe, S["node_summed"], t - 1)
                for k in range(KC):
                    last = nc.tensor.transpose(banks[0:NODES, h, k * P:(k + 1) * P], x_turned_sb[:, h, k, :],
                                               ident[:, :])
                last.then_inc(S["win_turned"], 1)

            def turn_g(t, h):
                pe.wait_ge(S["g_ready"], t + 1)
                wait_count(pe, S["g_back"], t - 1)
                for k in range(KC):
                    last = nc.tensor.transpose(banks[:, 2 + h, k * NODES:(k + 1) * NODES],
                                               g_t[:, h, k * P:(k + 1) * P], ident[0:NODES, 0:NODES])
                last.then_inc(S["g_turned"], 1)

            pe.wait_ge(S["agg_added"], NG)
            for turn_stage in (turn_win, turn_g):
                for h in range(2):
                    turn_stage(h, h)
                with pe.Fori(1, NN // 2) as i:
                    for h in range(2):
                        turn_stage(2 * i + h, h)

            def hop_steps(k, scatter_stage):
                def rows_of(u):
                    return gathered[:, u // TILES, u % TILES, 0:H]

                def are_gathered(turn, u, t):
                    if u % TILES == 0:
                        pe.wait_ge(S[f"h{k}_gathered{u // TILES}"], 16 * TILES * (turn + 1))

                def step(i, u):
                    scatter_stage(rows_of, are_gathered, f"h{k}_", *ahead(i, u, 0))
                over_tiles(pe, step, 0, NT, R)

            for k in range(2):
                with pe.If(in_order):
                    hop_steps(k, scatter)
                with pe.Else():
                    hop_steps(k, scatter_anywhere)
                if k == 0:
                    def turn_hop(t, h):
                        pe.wait_ge(S["hop_scaled"], t + 1)
                        wait_count(pe, S["hop_ready"], t - 1)
                        for c in range(KC):
                            last = nc.tensor.transpose(banks[0:NODES, h, c * P:(c + 1) * P], x_turned_sb[:, h, c, :],
                                                       ident[:, :])
                        last.then_inc(S["hop_turned"], 1)

                    for h in range(2):
                        turn_hop(h, h)
                    with pe.Fori(1, NN // 2) as i:
                        for h in range(2):
                            turn_hop(2 * i + h, h)

            def logits(t, h):
                pe.wait_ge(S["win_copied"], NN + t + 1)
                wait_count(pe, S["l_chain"], t - 1)
                for k in range(KC):
                    last = nc.tensor.matmul(banks[0:NODES, h, 0:H], x_turned_sb[:, h, k, :], w_l_turned[:, k, :],
                                            start=k == 0, stop=k == KC - 1)
                last.then_inc(S["logits_done"], 1)

            for h in range(2):
                logits(h, h)
            with pe.Fori(1, NN // 2) as i:
                for h in range(2):
                    logits(2 * i + h, h)

        @block.scalar
        def _(act):
            def copy_x(i, h):
                t = 2 * i + h
                act.wait_ge(S["xa_turned"], t + 1)
                wait_count(act, S["p_product"], t - 1)
                nc.scalar.copy(x_turned_sb[:, h, :, :].rearrange("p k n -> p (k n)"),
                               banks[:, h, 0:KC * NODES]).then_inc(S["xa_ready"], 1)

            for h in range(2):
                copy_x(0, h)
            with act.Fori(1, NN // 2) as i:
                for h in range(2):
                    copy_x(i, h)

            act.wait_ge(S["deg_made"], 1)
            nc.scalar.activation(dinv_rows[:, :], dinv_rows[:, :], ACT.Sqrt).then_inc(S["deg_rooted"], 1)

            def copy_index(index, gathered, turn, s):
                if isinstance(turn, int) and turn >= R:
                    return
                wait_count(act, S[f"{gathered}{s}"], 16 * TILES * turn)
                c = STEP * turn + TILES * s
                columns = src_t[:, c:c + TILES] if isinstance(c, int) else src_t[:, ds(c, TILES)]
                nc.scalar.copy(index_now[:, s, :], columns).then_inc(S[index], 1)

            def copy_ea(turn, s):
                g = 2 * turn + s
                if isinstance(g, int) and not 0 <= g < NG:
                    return
                act.wait_ge(S["ea_turned"], g + 1)
                wait_count(act, S["edge_product"], TILES * (g - 1))
                nc.scalar.copy(ea_turned_sb[:, s, :], banks[:, 7, :]).then_inc(S["ea_ready"], 1)

            def activate(turn, u, t):
                if isinstance(t, int) and not 0 <= t < NT:
                    return
                act.wait_ge(S["pre_ready"], t + 1)
                wait_count(act, S["msg_ready"], t - 1)
                nc.scalar.activation(gate[:, u % 2, :], pre[:, u % 2, H:H2], ACT.Sigmoid).then_inc(S["gate_ready"], 1)
                act.wait_ge(S["pre_turned"], t + 1)
                wait_count(act, S["core_done"], t - 1)
                nc.scalar.activation(hidden[:, u % 2, :, :].rearrange("p k n -> p (k n)"), banks[:, 2 + u % 2, 0:H],
                                     ACT.Relu).then_inc(S["hidden_ready"], 1)

            def step(i, u):
                activate(*ahead(i, u, 1))
                if u % TILES == 0:
                    turn, place, _ = ahead(i, u, TILES)
                    copy_ea(turn, place // TILES)
                    if not (isinstance(i, int) and i < 0):
                        copy_index("p_index", "p_gathered", i + 1, u // TILES)

            act.wait_ge(S["tables_copied"], 4)
            for s in range(2):
                copy_index("p_index", "p_gathered", 0, s)
            over_tiles(act, step, -TILES, NT, R)

            def copy_win(t, h, before):
                wait_count(act, S["win_turned" if before == 0 else "logits_done"], t - 1)
                nc.scalar.copy(x_turned_sb[:, h, :, :], node_cols(agg, t)).then_inc(S["win_copied"], 1)

            def scale_g(t, h):
                act.wait_ge(S["x3_ready"], t + 1)
                wait_count(act, S["g_turned"], t - 1)
                wait_count(act, S[f"g_stored{h}"], 8 * (t - h))
                scale = dinv_col[:, t:t + 1] if isinstance(t, int) else dinv_col[:, ds(t, 1)]
                rows = x3[:, t, :] if isinstance(t, int) else x3[:, ds(t, 1), :].rearrange("p a n -> p (a n)")
                nc.scalar.activation(g_t[:, h, :], rows, ACT.Copy, scale=scale).then_inc(S["g_ready"], 1)

            def back_g(t, h):
                act.wait_ge(S["g_turned"], t + 1)
                nc.scalar.copy(node_cols(agg, t), banks[:, 2 + h, 0:KC * NODES].rearrange("p (k n) -> p k n", k=KC)
                               ).then_inc(S["g_back"], 1)

            def deviation(n):
                act.wait_ge(S["variances_ready"], n + 1)
                nc.scalar.activation(rstd[:, n, :], rstd[:, n, :], ACT.Sqrt).then_inc(S["deviations_ready"], 1)

            act.wait_ge(S["agg_added"], NG)
            for h in range(2):
                copy_win(h, h, 0)
            with act.Fori(1, NN // 2) as i:
                for h in range(2):
                    copy_win(2 * i + h, h, 0)
            deviation(0)
            deviation(1)
            act.wait_ge(S["dinv_loaded"], 32)
            for h in range(2):
                scale_g(h, h)
            with act.Fori(1, NN // 2) as i:
                for h in range(2):
                    back_g(2 * i + h - 2, h)
                    scale_g(2 * i + h, h)
            for h in range(2):
                back_g(NN - 2 + h, h)

            for s in range(2):
                copy_index("h0_index", "h0_gathered", 0, s)
            with act.Fori(1, R) as i:
                for s in range(2):
                    copy_index("h0_index", "h0_gathered", i, s)

            def copy_hop(t, h):
                act.wait_ge(S["hop_turned"], t + 1)
                wait_count(act, S[f"hop_stored{h}"], 8 * (t - h))
                nc.scalar.copy(g_t[:, h, :], banks[0:NODES, h, 0:H]).then_inc(S["hop_ready"], 1)

            for h in range(2):
                act.wait_ge(S[f"g_stored{h}"], 8 * NN)
            for h in range(2):
                copy_hop(h, h)
            with act.Fori(1, NN // 2) as i:
                for h in range(2):
                    copy_hop(2 * i + h, h)

            for s in range(2):
                copy_index("h1_index", "h1_gathered", 0, s)
            with act.Fori(1, R) as i:
                for s in range(2):
                    copy_index("h1_index", "h1_gathered", i, s)

            def exponentials(t, h):
                act.wait_ge(S["l_chain"], t + 1)
                wait_count(act, S["y_summed"], t - 1)
                nc.scalar.activation(expo[:, :], node[:, h, :], ACT.Exp, bias=top[:, h, 1:2],
                                     accum_out=sums[:, h:h + 1]).then_inc(S["expd"], 1)
                act.wait_ge(S["expd"], t + 1)
                nc.scalar.activation(lse[:, h:h + 1], sums[:, h:h + 1], ACT.Ln).then_inc(S["logd"], 1)

            act.wait_ge(S["h1_agg_added"], NG)
            for h in range(2):
                copy_win(h, h, 1)
            for h in range(2):
                exponentials(h, h)
                copy_win(2 + h, h, 1)
            with act.Fori(2, NN // 2) as i:
                for h in range(2):
                    exponentials(2 * i + h - 2, h)
                    copy_win(2 * i + h, h, 1)
            for h in range(2):
                exponentials(NN - 2 + h, h)
            deviation(2)

        @block.vector
        def _(dve):
            done = [0]

            def then(instruction):
                done[0] += 1
                instruction.then_inc(S["self_dve"], 1)
                dve.wait_ge(S["self_dve"], done[0])

            dve.wait_ge(S["setup_loaded"], 16 * setup_dmas[0])
            nc.vector.tensor_copy(dst_f[0:R, :, :], dst_rows[0:R, :, :])
            nc.vector.tensor_copy(index_rows[0:R, 0, :, :], src_rows[0:R, :, :])
            nc.vector.tensor_single_scalar(hi_i[0:R, :, :], dst_rows[0:R, :, :], WINDOW.bit_length() - 1,
                                           ALU.arith_shift_right)
            then(nc.vector.tensor_single_scalar(lo_i[0:R, :, :], dst_rows[0:R, :, :], WINDOW - 1, ALU.bitwise_and))
            nc.vector.tensor_copy(index_rows[0:R, 2, :, :], hi_i[0:R, :, :])
            nc.vector.tensor_copy(index_rows[0:R, 3, :, :], lo_i[0:R, :, :])
            nc.vector.tensor_reduce(base_f[0:R, :], dst_f[0:R, :, :], AX.X, ALU.min)
            then(nc.vector.tensor_reduce(top_f[0:R, :], dst_f[0:R, :, :], AX.X, ALU.max))
            then(nc.vector.tensor_tensor(span_f[0:R, :], top_f[0:R, :], base_f[0:R, :], ALU.subtract))
            then(nc.vector.tensor_reduce(span_max[0:R, :], span_f[0:R, :], AX.X, ALU.max))
            nc.vector.tensor_tensor(index_rows[0:R, 1, :, :], dst_f[0:R, :, :],
                                    base_f[0:R, :].unsqueeze(2).to_broadcast([R, 2, GROUP]),
                                    ALU.subtract).then_inc(S["rows_made"], 1)
            dve.wait_ge(S["iota_made"], 3)
            nc.vector.tensor_copy(block_starts[:, :], block_i[:, :])
            nc.vector.tensor_copy(iota[:, :], iota_i[:, :])
            nc.vector.tensor_copy(iota_b[:, :], iota_i[:, :])
            then(nc.vector.tensor_copy(w_e_hi[:, :], w_e[:, :]))
            nc.vector.tensor_tensor(w_e_lo[:, :], w_e[:, :], w_e_hi[:, :].bitcast(F32), ALU.subtract).then_inc(
                S["w_split"], 1)
            dve.wait_ge(S["w_turned"], 1)
            nc.vector.tensor_copy(w_l_turned[:, :, :].rearrange("p k n -> p (k n)"), banks[:, 5, :]).then_inc(
                S["w_copied"], 1)
            for n, table in enumerate((src_t, local_t, hi_t, lo_t)):
                dve.wait_ge(S["tables_turned"], n + 1)
                by_tile = table[:, :].rearrange("p (i s j) -> p i s j", s=2, j=TILES)
                for s in range(2):
                    last = nc.vector.tensor_copy(by_tile[:, :, s, :],
                                                 banks[:, 6 + s, 0:TILES * R].rearrange("p (j i) -> p i j", j=TILES))
                last.then_inc(S["tables_copied"], 1)
            dve.wait_ge(S["tables_copied"], 4)
            dve.wait_ge(S["base_turned"], 1)
            nc.vector.tensor_copy(bases[:, :], banks[0:2, 4, 0:R])
            then(nc.vector.tensor_reduce(widest[:, :], banks[0:1, 4, P:P + R], AX.X, ALU.max))
            nc.vector.tensor_single_scalar(fits[:, :], widest[:, :], float(WINDOW), ALU.is_lt).then_inc(S["fits_known"], 1)

            def bias_p(i, h):
                t = 2 * i + h
                dve.wait_ge(S["p_product"], t + 1)
                wait_count(dve, S[f"p_stored{h}"], 8 * (t - h))
                nc.vector.tensor_tensor(p_t[:, h, :], banks[0:NODES, 2 + h, :], bias_in[0:NODES, :],
                                        ALU.add).then_inc(S["p_ready"], 1)

            for h in range(2):
                bias_p(0, h)
            with dve.Fori(1, NN // 2) as i:
                for h in range(2):
                    bias_p(i, h)

            def column(table, t):
                return table[:, t:t + 1] if isinstance(t, int) else table[:, ds(t, 1)]

            def degree_hot(i, u):
                t = STEP * i + u
                wait_count(dve, S["deg_counted"], t - STEP + 1)
                nc.vector.tensor_single_scalar(hot_hi[:, u, :], iota_b[:, 0:NB], column(hi_t, t), ALU.is_equal)
                nc.vector.tensor_single_scalar(hot_lo[:, u, :], iota_b[:, :], column(lo_t, t), ALU.is_equal).then_inc(
                    S["deg_hot"], 1)

            over_tiles(dve, degree_hot, 0, NT, R)
            dve.wait_ge(S["deg_counted"], NT)
            nc.vector.tensor_single_scalar(dinv_rows[:, :], banks[0:NB, 4, 0:P], 1.0, ALU.add).then_inc(
                S["deg_made"], 1)

            dst_t = hi_t
            then(nc.vector.scalar_tensor_tensor(out=dst_t[:, :], in0=hi_t[:, :], scalar=float(WINDOW), in1=lo_t[:, :],
                                                op0=ALU.mult, op1=ALU.add))

            dve.wait_ge(S["deg_rooted"], 1)
            nc.vector.reciprocal(dinv_rows[:, :], dinv_rows[:, :]).then_inc(S["dinv_made"], 1)

            def split_ea(turn, s):
                g = 2 * turn + s
                if isinstance(g, int) and not 0 <= g < NG:
                    return
                dve.wait_ge(S[f"ea_loaded{s}"], 16 * (turn + 1))
                wait_count(dve, S["ea_turned"], g)
                nc.vector.tensor_copy(ea_parts[:, :, 0, :], ea[:, s, :, :]).then_inc(S["ea_rounded"], 1)
                dve.wait_ge(S["ea_rounded"], g + 1)
                nc.vector.tensor_tensor(ea_parts[:, :, 1, :], ea[:, s, :, :], ea_parts[:, :, 0, :].bitcast(F32),
                                        ALU.subtract).then_inc(S["ea_split"], 1)

            def add_product(turn, u, t):
                if isinstance(t, int) and not 0 <= t < NT:
                    return
                s, j = u // TILES, u % TILES
                dve.wait_ge(S["edge_product"], t + 1)
                if j == 0:
                    dve.wait_ge(S[f"p_gathered{s}"], 16 * TILES * (turn + 1))
                wait_count(dve, S["pre_turned"], t - 1)
                wait_count(dve, S["gate_ready"], t - 1)
                nc.vector.tensor_tensor(pre[:, u % 2, :], banks[:, u % 2, :], gathered[:, s, j, :],
                                        ALU.add).then_inc(S["pre_ready"], 1)

            def message(turn, u, t):
                if isinstance(t, int) and not 0 <= t < NT:
                    return
                dve.wait_ge(S["core_done"], t + 1)
                wait_count(dve, S["msg_ready"], t)
                nc.vector.tensor_tensor(core[:, :], banks[:, 4 + u % 2, 0:H], bias_core[:, :], ALU.add).then_inc(
                    S["core_biased"], 1)
                dve.wait_ge(S["core_biased"], t + 1)
                dve.wait_ge(S["gate_ready"], t + 1)
                wait_count(dve, S["scattered"], t - STEP + 1)
                nc.vector.tensor_tensor(msg[:, u, :], core[:, :], gate[:, u % 2, :], ALU.mult).then_inc(
                    S["msg_ready"], 1)

            def one_hot(hop, turn, u, t):
                if isinstance(t, int) and not 0 <= t < NT:
                    return
                wait_count(dve, S[hop + "scattered"], t - STEP + 1)
                nc.vector.tensor_single_scalar(hot[:, u, :], iota[:, 0:WINDOW], column(local_t, t),
                                               ALU.is_equal).then_inc(S[hop + "hot_ready"], 1)

            def add_window(hop, turn, u, t):
                if isinstance(t, int) and not 0 <= t < NT:
                    return
                s, g = u // TILES, 2 * turn + u // TILES
                if u % TILES < TILES - 1:
                    return
                at = bases[s:s + 1, turn:turn + 1] if isinstance(turn, int) else bases[s:s + 1, ds(turn, 1)]
                base = dve.value_load(at, min_val=0, max_val=N - 1)
                dve.wait_ge(S[hop + "scattered"], TILES * (g + 1))
                wait_count(dve, S[hop + "agg_added"], g)
                where = agg[:, :, ds(base, WINDOW)]
                nc.vector.tensor_tensor(where, where, banks[:, 6, 0:KC * WINDOW].rearrange("p (k n) -> p k n", k=KC),
                                        ALU.add).then_inc(S[hop + "agg_added"], 1)

            def no_one_hot(hop, turn, u, t):
                pass

            def add_anywhere(hop, turn, u, t):
                if isinstance(t, int) and not 0 <= t < NT:
                    return
                s, j, g = u // TILES, u % TILES, 2 * turn + u // TILES
                if j < TILES - 1:
                    return
                with dve.Fori(0, NB) as w:
                    dve.wait_ge(S[hop + "slow_added"], g * NB + w + 1)
                    for jj in range(TILES):
                        last = nc.vector.tensor_scalar(hot[:, TILES * s + jj, :], iota[:, 0:WINDOW],
                                                       column(dst_t, t - j + jj), block_starts[:, ds(w, 1)],
                                                       ALU.subtract, ALU.is_equal)
                    last.then_inc(S[hop + "slow_hot"], 1)
                    dve.wait_ge(S[hop + "slow_scattered"], g * NB + w + 1)
                    where = agg[:, :, ds(WINDOW * w, WINDOW)]
                    nc.vector.tensor_tensor(where, where,
                                            banks[:, 6, 0:KC * WINDOW].rearrange("p (k n) -> p k n", k=KC),
                                            ALU.add).then_inc(S[hop + "slow_added"], 1)
                dve.wait_ge(S[hop + "slow_added"], (g + 1) * NB + 1)
                dve.sem_inc(S[hop + "agg_added"], 1)

            def edge_steps(hot_stage, add_stage):
                def step(i, u):
                    hot_stage("", *ahead(i, u, 0))
                    add_product(*ahead(i, u, 2))
                    message(*ahead(i, u, 0))
                    add_stage("", *ahead(i, u, -1))
                    if u % TILES == 2:
                        turn, place, _ = ahead(i, u, TILES + 2)
                        split_ea(turn, place // TILES)
                over_tiles(dve, step, -TILES - 2, NT + 1, R)

            def hop_steps(hop, hot_stage, add_stage):
                def step(i, u):
                    if u % TILES == 0:
                        for j in range(TILES):
                            hot_stage(hop, *ahead(i, u, TILES + j))
                    add_stage(hop, *ahead(i, u, 0))
                over_tiles(dve, step, -TILES, NT, R)

            in_order = dve.value_load(fits[0:1, 0:1], min_val=0, max_val=1)
            dve.wait_ge(S["agg_cleared"], 1)
            with dve.If(in_order):
                edge_steps(one_hot, add_window)
            with dve.Else():
                dve.sem_inc(S["slow_added"], 1)
                edge_steps(no_one_hot, add_anywhere)

            def x3_rows(t):
                return x3[:, t, :] if isinstance(t, int) else x3[:, ds(t, 1), :].rearrange("p a n -> p (a n)")

            def sum_with_stats(n, t, h, summed, sum_rows):
                wait_count(dve, S["stats_ready"], n * NN + t)
                wait_count(dve, S["moments_ready"], n * NN + t - 1)
                sum_rows().then_inc(S[summed], 1)
                if not isinstance(t, int) or t >= 1:
                    put_together(1 - h)
                dve.wait_ge(S[summed], t + 1)
                if not isinstance(t, int) or t >= 2:
                    keep_moments(n, t - 2, h)
                nc.vector.bn_stats(stats[:, h, :], x3_rows(t)).then_inc(S["stats_ready"], 1)

            def put_together(h):
                nc.vector.bn_aggr(moments_now[:, h, :], stats[:, h, :]).then_inc(S["moments_ready"], 1)

            def keep_moments(n, t, h):
                to = moments[:, n, t, :] if isinstance(t, int) else moments[:, n, ds(t, 1), :].rearrange("p a m -> p (a m)")
                return nc.vector.tensor_copy(to, moments_now[:, h, :])

            def reciprocal_deviations(n):
                dve.wait_ge(S["stats_ready"], (n + 1) * NN)
                put_together(1)
                dve.wait_ge(S["moments_ready"], (n + 1) * NN)
                keep_moments(n, NN - 2, 0)
                keep_moments(n, NN - 1, 1).then_inc(S["moments_kept"], 1)
                dve.wait_ge(S["moments_kept"], n + 1)
                nc.vector.tensor_single_scalar(rstd[:, n, :], moments[:, n, :, 1], EPS, ALU.add).then_inc(
                    S["variances_ready"], 1)
                dve.wait_ge(S["deviations_ready"], n + 1)
                nc.vector.reciprocal(rstd[:, n, :], rstd[:, n, :]).then_inc(S["rstd_ready"], 1)
                dve.wait_ge(S["rstd_ready"], n + 1)

            def normalise(n, t, result):
                mean = moments[:, n, t, 0:1] if isinstance(t, int) else moments[:, n, ds(t, 1), 0]
                return nc.vector.tensor_scalar(result, x3_rows(t), mean, column(rstd[:, n, :], t),
                                               ALU.subtract, ALU.mult)

            def over_nodes(stage):
                for h in range(2):
                    stage(h, 0, h)
                with dve.Fori(1, NN // 2) as i:
                    for h in range(2):
                        stage(2 * i + h, i, h)

            def first_sum(t, i, h):
                dve.wait_ge(S["win_turned"], t + 1)
                dve.wait_ge(S[f"xn_loaded{h}"], 16 * (i + 1))
                sum_with_stats(0, t, h, "node_summed", lambda: nc.vector.tensor_tensor(
                    x3_rows(t), banks[0:NODES, h, 0:H], x_t[:, h, :], ALU.add))

            def first_norm(t, i, h):
                rows = node[:, h, :]
                normalise(0, t, rows).then_inc(S["first_normed"], 1)
                dve.wait_ge(S["first_normed"], t + 1)
                nc.vector.tensor_tensor(rows, rows, gamma_all[0:NODES, :], ALU.mult).then_inc(S["first_scaled"], 1)
                dve.wait_ge(S["first_scaled"], t + 1)
                dve.wait_ge(S["xb_ready"], t + 1)
                sum_with_stats(1, t, h, "first_summed", lambda: nc.vector.tensor_tensor(
                    x3_rows(t), rows, xb_t[:, h, :], ALU.add))

            def second_norm(t, i, h):
                normalise(1, t, x3_rows(t)).then_inc(S["x3_ready"], 1)

            over_nodes(first_sum)
            reciprocal_deviations(0)
            over_nodes(first_norm)
            reciprocal_deviations(1)
            over_nodes(second_norm)

            dve.wait_ge(S["dinv_loaded"], 32)
            nc.vector.tensor_tensor(dinv_all[:, :], dinv_all[:, :], dinv_all[:, :], ALU.mult).then_inc(
                S["dinv_squared"], 1)
            dve.wait_ge(S["g_back"], NN)
            for k in range(2):
                hop = f"h{k}_"
                with dve.If(in_order):
                    hop_steps(hop, one_hot, add_window)
                with dve.Else():
                    dve.sem_inc(S[hop + "slow_added"], 1)
                    hop_steps(hop, no_one_hot, add_anywhere)
                if k == 0:
                    def scale_hop(t, h):
                        wait_count(dve, S["hop_turned"], t - 1)
                        wait_count(dve, S["hop_back"], t - 1)
                        cols = (dinv_all[:, NODES * t:NODES * (t + 1)] if isinstance(t, int)
                                else dinv_all[:, ds(NODES * t, NODES)])
                        nc.vector.tensor_tensor(x_turned_sb[:, h, :, :], node_cols(agg, t),
                                                cols.unsqueeze(1).to_broadcast([P, KC, NODES]), ALU.mult).then_inc(
                            S["hop_scaled"], 1)

                    dve.wait_ge(S["h0_agg_added"], NG)
                    dve.wait_ge(S["dinv_squared"], 1)
                    for h in range(2):
                        scale_hop(h, h)
                    with dve.Fori(1, NN // 2) as i:
                        for h in range(2):
                            scale_hop(2 * i + h, h)
                    dve.wait_ge(S["hop_back"], NN)

            def logit_rows(t, h):
                rows = node[:, h, :]
                dve.wait_ge(S["logits_done"], t + 1)
                nc.vector.scalar_tensor_tensor(out=rows, in0=banks[0:NODES, h, 0:H], scalar=column(dinv_col, t),
                                               in1=bias_l[0:NODES, :], op0=ALU.mult, op1=ALU.add).then_inc(
                    S["logit_rows"], 1)
                dve.wait_ge(S["logit_rows"], t + 1)
                nc.vector.tensor_reduce(top[:, h, 0:1], rows, AX.X, ALU.max).then_inc(S["logit_top"], 1)
                dve.wait_ge(S["logit_top"], t + 1)
                nc.vector.tensor_single_scalar(top[:, h, 1:2], top[:, h, 0:1], -1.0, ALU.mult).then_inc(S["l_chain"], 1)

            def last_sum(t, h):
                rows = node[:, h, :]
                dve.wait_ge(S["logd"], t + 1)
                nc.vector.tensor_scalar(rows, rows, top[:, h, 0:1], lse[:, h:h + 1], ALU.subtract,
                                        ALU.subtract).then_inc(S["log_softmax"], 1)
                dve.wait_ge(S["log_softmax"], t + 1)
                sum_with_stats(2, t, h, "y_summed", lambda: nc.vector.tensor_tensor(
                    x3_rows(t), rows, x3_rows(t), ALU.add))

            def last_norm(t, i, h):
                wait_count(dve, S[f"y_stored{h}"], 8 * (t - h))
                normalise(2, t, y_t[:, h, :]).then_inc(S["y_ready"], 1)

            for h in range(2):
                logit_rows(h, h)
            for h in range(2):
                last_sum(h, h)
                logit_rows(2 + h, h)
            with dve.Fori(2, NN // 2) as i:
                for h in range(2):
                    last_sum(2 * i + h - 2, h)
                    logit_rows(2 * i + h, h)
            for h in range(2):
                last_sum(NN - 2 + h, h)
            reciprocal_deviations(2)
            over_nodes(last_norm)


_INS = ["x", "src", "dst", "edge_attr_64", "L0_gnn_W1", "L0_gnn_b1", "L0_gnn_W2", "L0_gnn_b2", "L0_gnn_Wg",
        "L0_gnn_bg", "L0_gnn_gamma", "L0_gnn_beta", "L1_gnn_W", "L1_gnn_b"]


def kernel(**inputs):
    import concourse.bacc as bacc
    from concourse.bass_utils import run_bass_kernel_spmd

    nc = bacc.Bacc("TRN2", target_bir_lowering=False, num_devices=1)
    arrays, args = {}, []
    for name in _INS:
        a = np.ascontiguousarray(inputs[name])
        arrays[f"in_{name}"] = a
        args.append(nc.dram_tensor(f"in_{name}", a.shape, mybir.dt.from_np(a.dtype), kind="ExternalInput").ap())
    out = nc.dram_tensor("out", inputs["x"].shape, F32, kind="ExternalOutput").ap()
    gnn_kernel(nc, *args, out)
    result = run_bass_kernel_spmd(nc, [arrays], core_ids=[0])
    return result.results[0]["out"]
```

```python
from contextlib import ExitStack

import numpy as np

import concourse.bass as bass
import concourse.mybir as mybir

P = 128
GROUP = 512
TILES = 4
WINDOW = 128
NODES = 125
STEP = 2 * TILES
HOP_SLOTS = 4
HOP_STEP = HOP_SLOTS * TILES
EPS = 1e-5

F32 = mybir.dt.float32
F32R = mybir.dt.float32r
BF16 = mybir.dt.bfloat16
I32 = mybir.dt.int32
ALU = mybir.AluOpType
ACT = mybir.ActivationFunctionType
AX = mybir.AxisListType
ds = bass.ds


def wait_count(engine, semaphore, count):
    if not isinstance(count, int) or count > 0:
        engine.wait_ge(semaphore, count)


def over_tiles(engine, step, first, last, turns, per=STEP):
    for t in range(first, per):
        step(t // per, t % per)
    with engine.Fori(1, turns - 1) as i:
        for u in range(per):
            step(i, u)
    for t in range(per * (turns - 1), last):
        step(t // per, t % per)


def over_setup(engine, step, turns):
    step(0)
    step(1)
    with engine.Fori(2, turns - 1) as i:
        step(i)
    step(turns - 1)


def ahead(i, u, lag, per=STEP):
    turn, place = i + (u + lag) // per, (u + lag) % per
    return turn, place, per * turn + place, per // TILES * turn + place // TILES


def gnn_kernel(nc, x, src, dst, edge_attr, W1, b1, W2, b2, Wg, bg, gamma, beta, Wl, bl, out):
    N, H = x.shape
    E, DE = edge_attr.shape
    KC = H // P
    H2 = 2 * H
    NG = -(-E // GROUP)
    R = NG // 2
    HR = NG // HOP_SLOTS
    NT = NG * TILES
    OVERLAP = NG * GROUP - E
    NN = N // NODES
    NB = -(-N // WINDOW)
    COUNTS = -(-R // (NN // 2))
    NCOL = N + WINDOW
    assert KC * P == H and 2 * DE == P and NG % HOP_SLOTS == 0 and R <= P and OVERLAP < GROUP
    assert NN * NODES == N and NN % 2 == 0 and NB <= P and H2 == 512 and HR > 2
    assert COUNTS % 2 == 0 and 0 <= R - COUNTS * (NN // 2 - 1) <= COUNTS

    p_table = nc.dram_tensor("p_table", (N, H2), F32, kind="Internal").ap()
    hop_table = [nc.dram_tensor(f"hop_table{k}", (N, H), F32, kind="Internal").ap() for k in range(2)]
    dinv_flat = nc.dram_tensor("dinv_flat", (NB * P,), F32, kind="Internal").ap()

    with ExitStack() as ctx:
        def sb(name, shape, dt=F32):
            return ctx.enter_context(nc.sbuf_tensor(name, shape, dt))

        def sem(name):
            return ctx.enter_context(nc.semaphore(name))

        banks = ctx.enter_context(nc.psum_tensor("banks", [P, 8, 512], F32))

        w_e_hi = sb("w_e_hi", [P, H2], F32R)
        w_e_lo = sb("w_e_lo", [P, H2], F32R)
        w_2 = sb("w_2", [P, KC, H])
        w_l_turned = sb("w_l_turned", [P, KC, H])
        bias_in = sb("bias_in", [P, H2])
        bias_core = sb("bias_core", [P, H])
        gamma_all = sb("gamma_all", [P, H])
        beta_all = sb("beta_all", [P, H])
        bias_l = sb("bias_l", [P, H])
        ident = sb("ident", [P, P])
        iota = sb("iota", [P, P])
        iota_b = sb("iota_b", [P, P], BF16)
        block_starts = sb("block_starts", [P, NB])

        pair = 2 * GROUP
        x3_room = sb("x3_room", [P, max(NN * H, 9 * pair)])
        x3 = x3_room[0:NODES, 0:NN * H].rearrange("p (t n) -> p t n", n=H)

        def rows_at(k, dt):
            return x3_room[:, k * pair:(k + 1) * pair].bitcast(dt).rearrange("p (s e) -> p s e", s=2)

        index_rows = x3_room[:, 0:4 * pair].rearrange("p (k s e) -> p k s e", k=4, s=2)
        dst_f = rows_at(4, F32)
        dst_rows, src_rows, hi_i, lo_i = (rows_at(k, I32) for k in range(5, 9))
        base_f = sb("base_f", [P, 2])
        top_f = sb("top_f", [P, 2])
        span_f = sb("span_f", [P, 2])
        span_max = sb("span_max", [P, 1])
        widest = sb("widest", [1, 1])
        fits = sb("fits", [1, 1], I32)
        bases = sb("bases", [2, R], I32)
        src_t = sb("src_t", [P, NT], I32)
        local_t = sb("local_t", [P, NT])
        hi_t = sb("hi_t", [P, NT])
        lo_t = sb("lo_t", [P, NT])

        agg = sb("agg", [P, KC, NCOL])
        dinv_all = sb("dinv_all", [P, N])
        dinv_col = sb("dinv_col", [NODES, NN])
        dinv_rows = sb("dinv_rows", [NB, P])

        hot = sb("hot", [P, STEP, WINDOW])
        gathered = sb("gathered", [P, 2, TILES, H2])
        start_room = gathered[:, :, :, :].rearrange("p s j n -> p (s j n)")
        w_e = start_room[:, 0:H2]
        w_l = start_room[:, H2:H2 + KC * H].rearrange("p (k n) -> p k n", k=KC)
        iota_i = start_room[:, 2 * H2:2 * H2 + P].bitcast(I32)
        block_i = start_room[:, 3 * H2:3 * H2 + NB].bitcast(I32)
        hop_rows = gathered[:, :, :, :].rearrange("p s j n -> p (s j n)").rearrange(
            "p (s j n) -> p s j n", s=HOP_SLOTS, j=TILES)
        index_now = sb("index_now", [P, HOP_SLOTS, TILES], I32)
        ea = sb("ea", [P, 2, TILES, DE])
        ea_parts = sb("ea_parts", [P, TILES, 2, DE], F32R)
        ea_turned_sb = sb("ea_turned_sb", [P, 2, GROUP], F32R)
        pre_room = sb("pre_room", [P, 2 * H2])
        pre = pre_room[:, :].rearrange("p (h n) -> p h n", h=2)
        hidden = sb("hidden", [P, 2, KC, P])
        hot_lo = pre_room[:, :].bitcast(BF16).rearrange("p (d u n) -> p d u n", d=2, u=STEP)
        hot_hi = hidden[:, :, :, :].rearrange("p h k n -> p (h k n)")[:, 0:STEP * NB].bitcast(BF16).rearrange(
            "p (d u n) -> p d u n", d=2, u=STEP)
        gate = sb("gate", [P, 2, H])
        core = sb("core", [P, H])
        room = sb("room", [P, STEP * H])
        w_x = room[:, 0:KC * H2].rearrange("p (k n) -> p k n", k=KC)
        p_t = room[0:NODES, KC * H2:KC * H2 + 2 * H2].rearrange("p (h n) -> p h n", h=2)
        msg = room[:, :].rearrange("p (u n) -> p u n", u=STEP)
        node, sum_t, g_t, expo = (room[0:NODES, k * 2 * H:(k + 1) * 2 * H].rearrange("p (h n) -> p h n", h=2)
                                  for k in range(4))
        y_t = sum_t
        x_t = sb("x_t", [NODES, 2, H])
        x_turned_sb = sb("x_turned_sb", [P, 2, KC, NODES])
        stats = sb("stats", [NODES, 2, 2, 6])
        moments = sb("moments", [NODES, 2, 2, 2])
        scale = sb("scale", [NODES, 2, 2])
        shift = sb("shift", [NODES, 2, 2])
        eps = sb("eps", [NODES, 1])
        top = sb("top", [NODES, 2, 2])
        sums = sb("sums", [NODES, NN])
        lse = sb("lse", [NODES, NN])

        names = """setup_loaded consts_ready iota_made rows_made tables_turned tables_copied w_turned
        w_copied w_split base_turned fits_known pool_masked self_dve
        xa_turned xa_ready p_product p_ready
        deg_hot deg_counted deg_made deg_rooted dinv_made dinv_stored dinv_loaded agg_cleared
        p_index ea_split ea_turned ea_ready edge_product pre_ready pre_turned hidden_ready gate_ready core_done
        core_biased msg_ready hot_ready scattered agg_added slow_hot slow_scattered slow_added
        win_copied win_turned x_loaded node_summed node_stats node_moments node_deviation node_scale node_shift
        node_normed beta_added gamma_scaled sum_ready sum_stats sum_moments sum_deviation sum_scale sum_shift
        x3_ready g_ready g_turned g_back begun gathers_begun slow_begun ea_rounded dinv_squared
        hop_scaled hop_turned hop_ready
        logits_done logit_rows logit_top l_chain expd lse_ready y_added
        y_summed y_stats y_moments y_deviation y_scale y_shift y_ready""".split()
        S = {n: sem(n) for n in names}
        for k in range(2):
            for n in "index hot_ready scattered agg_added slow_hot slow_scattered slow_added".split():
                S[f"h{k}_{n}"] = sem(f"h{k}_{n}")
            for n in ("p_gathered", "ea_loaded", "p_stored", "g_stored", "hop_stored", "y_stored", "xa_loaded"):
                S[f"{n}{k}"] = sem(f"{n}{k}")
            for s in range(HOP_SLOTS):
                S[f"h{k}_gathered{s}"] = sem(f"h{k}_gathered{s}")

        def count_turns(i, half):
            first = COUNTS * i + half * (COUNTS // 2)
            return [d for d in (first + k for k in range(COUNTS // 2)) if not isinstance(d, int) or d < R]

        def tile_columns(table, d):
            return table[:, STEP * d:STEP * (d + 1)] if isinstance(d, int) else table[:, ds(STEP * d, STEP)]

        setup_dmas = [0]
        block = ctx.enter_context(nc.Block())

        def over_nodes(engine, step, first, last):
            for t in range(first, 6):
                step(t // 2, t % 2)
            with engine.Fori(3, NN // 2 - 1) as i:
                for u in range(2):
                    step(i, u)
            for t in range(NN - 2, last):
                step(t // 2, t % 2)

        def at_tile(stage, i, u, lag):
            turn, place = i + (u + lag) // 2, (u + lag) % 2
            if not isinstance(turn, int) or 0 <= 2 * turn + place < NN:
                stage(2 * turn + place, place)

        def x3_rows(t):
            return x3[:, t, :] if isinstance(t, int) else x3[:, ds(t, 1), :].rearrange("p a n -> p (a n)")

        def column(table, t):
            return table[:, t:t + 1] if isinstance(t, int) else table[:, ds(t, 1)]

        def node_rows(table, t):
            return table[ds(NODES * t, NODES), :] if not isinstance(t, int) else table[NODES * t:NODES * (t + 1), :]

        def node_cols(table, t):
            return table[:, :, ds(NODES * t, NODES)] if not isinstance(t, int) else table[:, :, NODES * t:NODES * (t + 1)]

        @block.sync
        def _(sp):
            def load(to, of):
                sp.dma_start(to, of).then_inc(S["setup_loaded"], 16)
                setup_dmas[0] += 1

            full = (R - 1) * 2 * GROUP
            for rows, index in ((dst_rows, dst), (src_rows, src)):
                load(rows[0:R - 1, :, :], index[0:full].rearrange("(r s e) -> r s e", s=2, e=GROUP))
                load(rows[R - 1:R, 0, :], index[full:full + GROUP].rearrange("(r e) -> r e", r=1))
                load(rows[R - 1:R, 1, :], index[E - GROUP:E].rearrange("(r e) -> r e", r=1))
            for n, w in enumerate((W1, Wg)):
                cols = slice(n * H, (n + 1) * H)
                load(w_x[:, :, cols], w[0:H, :].rearrange("(k p) n -> p k n", p=P))
                load(w_e[0:DE, cols], w[H:H + DE, :])
                load(w_e[DE:P, cols], w[H:H + DE, :])
            load(bias_in[:, 0:H], b1.partition_broadcast(P))
            load(bias_in[:, H:H2], bg.partition_broadcast(P))
            load(w_2[:, :, :], W2.rearrange("(k p) n -> p k n", p=P))
            load(w_l[:, :, :], Wl.rearrange("(k p) n -> p k n", p=P))
            for to, of in ((bias_core, b2), (gamma_all, gamma), (beta_all, beta), (bias_l, bl)):
                load(to[:, :], of.partition_broadcast(P))

            def load_xa(i, h):
                t = 2 * i + h
                wait_count(sp, S["xa_turned"], t - 1)
                sp.dma_start(x_t[:, h, :], node_rows(x, t)).then_inc(S[f"xa_loaded{h}"], 16)

            for h in range(2):
                load_xa(0, h)
            with sp.Fori(1, NN // 2) as i:
                for h in range(2):
                    load_xa(i, h)

            sp.wait_ge(S["dinv_made"], 1)
            sp.dma_start(dinv_flat.rearrange("(b n) -> b n", n=P), dinv_rows[:, :]).then_inc(S["dinv_stored"], 16)
            sp.wait_ge(S["dinv_stored"], 16)
            with nc.allow_non_contiguous_dma("once, a few thousand words"):
                sp.dma_start(dinv_col[:, :], dinv_flat[0:N].rearrange("(t p) -> p t", p=NODES)).then_inc(
                    S["dinv_loaded"], 16)
            sp.dma_start(dinv_all[:, :], dinv_flat[0:N].partition_broadcast(P)).then_inc(S["dinv_loaded"], 16)

            sp.wait_ge(S["tables_turned"], 4)
            PART = NN // 5
            for t in range(0, NN, PART):
                sp.dma_start(x3[:, t:t + PART, :], x[NODES * t:NODES * (t + PART), :].rearrange(
                    "(t p) n -> p t n", p=NODES)).then_inc(S["x_loaded"], 16)

            def load_ea(i, s):
                g = 2 * i + s
                wait_count(sp, S["ea_split"], g - 1)
                if isinstance(g, int):
                    e0 = min(GROUP * g, E - GROUP)
                    rows = edge_attr[e0:e0 + GROUP, :]
                else:
                    rows = edge_attr[ds(GROUP * g, GROUP), :]
                sp.dma_start(ea[:, s, :, :], rows.rearrange("(p j) d -> p j d", j=TILES)).then_inc(
                    S[f"ea_loaded{s}"], 16)

            for s in range(2):
                load_ea(0, s)
            with sp.Fori(1, R - 1) as i:
                for s in range(2):
                    load_ea(i, s)
            for s in range(2):
                load_ea(R - 1, s)

            for table, ready, stored in ((hop_table[0], "g_ready", "g_stored"), (hop_table[1], "hop_ready", "hop_stored")):
                def store_rows(i, h):
                    t = 2 * i + h
                    sp.wait_ge(S[ready], t + 1)
                    sp.dma_start(node_rows(table, t), g_t[:, h, :]).then_inc(S[f"{stored}{h}"], 16)

                with sp.Fori(0, NN // 2) as i:
                    for h in range(2):
                        store_rows(i, h)

            def store_y(i, h):
                t = 2 * i + h
                sp.wait_ge(S["y_ready"], t + 1)
                sp.dma_start(node_rows(out, t), y_t[:, h, :]).then_inc(S[f"y_stored{h}"], 16)

            with sp.Fori(0, NN // 2) as i:
                for h in range(2):
                    store_y(i, h)
            for h in range(2):
                sp.wait_ge(S[f"y_stored{h}"], 8 * NN)

        @block.gpsimd
        def _(pool):
            nc.gpsimd.memset(ident[:, :], 0.0).then_inc(S["iota_made"], 1)
            nc.gpsimd.iota(iota_i[:, :], pattern=[[1, P]], base=0, channel_multiplier=0).then_inc(S["iota_made"], 1)
            nc.gpsimd.iota(block_i[:, :], pattern=[[-WINDOW, NB]], base=0, channel_multiplier=0).then_inc(
                S["iota_made"], 1)
            pool.wait_ge(S["iota_made"], 3)
            nc.gpsimd.affine_select(out=ident[:, :], in_=ident[:, :], compare_op=ALU.not_equal, fill=1.0, base=0,
                                    pattern=[[-1, P]], channel_multiplier=1).then_inc(S["consts_ready"], 1)
            nc.gpsimd.memset(eps[:, :], EPS).then_inc(S["consts_ready"], 1)
            nc.gpsimd.memset(agg[:, :, :], 0.0).then_inc(S["agg_cleared"], 1)

            pool.wait_ge(S["rows_made"], 1)
            if OVERLAP:
                for table in (1, 2):
                    rows = index_rows[0:R, table, 1, :]
                    nc.gpsimd.affine_select(
                        out=rows, in_=rows, compare_op=ALU.is_ge, fill=-1.0, base=(R - 1) * 2 * GROUP - OVERLAP,
                        pattern=[[1, GROUP]], channel_multiplier=-2 * GROUP).then_inc(S["pool_masked"], 1)

            def gather(table, rows, slots, stored, index, done, free, i, s):
                g = slots * i + s
                wait_count(pool, S[free], TILES * (g - slots + 1))
                if isinstance(g, int) and g == 0:
                    for h in range(2):
                        pool.wait_ge(S[f"{stored}{h}"], 8 * NN)
                pool.wait_ge(S[index], g + 1)
                pool.sem_inc(S["gathers_begun"], 1)
                for j in range(TILES):
                    pool.indirect_dma_start(
                        out=rows[:, s, j, :], out_offset=None, in_=table[:, :],
                        in_offset=bass.IndirectOffsetOnAxis(ap=index_now[:, s, j:j + 1], axis=0),
                    ).then_inc(S[f"{done}{s}"], 16)

            def gather_all(table, rows, slots, stored, index, done, free):
                for s in range(slots):
                    gather(table, rows, slots, stored, index, done, free, 0, s)
                with pool.Fori(1, NG // slots) as i:
                    for s in range(slots):
                        gather(table, rows, slots, stored, index, done, free, i, s)

            gather_all(p_table, gathered, 2, "p_stored", "p_index", "p_gathered", "pre_ready")

            def add_beta(t, h):
                pool.wait_ge(S["node_summed"], t + 1)
                nc.gpsimd.tensor_tensor(x3_rows(t), x3_rows(t), beta_all[0:NODES, :], ALU.add).then_inc(
                    S["beta_added"], 1)

            def scale_gamma(t, h):
                pool.wait_ge(S["node_normed"], t + 1)
                nc.gpsimd.tensor_tensor(node[:, h, :], node[:, h, :], gamma_all[0:NODES, :], ALU.mult).then_inc(
                    S["gamma_scaled"], 1)

            def node_step(i, u):
                at_tile(scale_gamma, i, u, -1)
                at_tile(add_beta, i, u, 0)

            over_nodes(pool, node_step, 0, NN + 1)

            gather_all(hop_table[0], hop_rows, HOP_SLOTS, "g_stored", "h0_index", "h0_gathered", "h0_scattered")

            gather_all(hop_table[1], hop_rows, HOP_SLOTS, "hop_stored", "h1_index", "h1_gathered", "h1_scattered")

        @block.tensor
        def _(pe):
            pe.wait_ge(S["consts_ready"], 1)
            pe.wait_ge(S["setup_loaded"], 16 * setup_dmas[0])

            for o in range(KC):
                for k in range(KC):
                    at = (k * KC + o) * P
                    last = nc.tensor.transpose(banks[:, 5, at:at + P], w_l[:, o, k * P:(k + 1) * P], ident[:, :])
            last.then_inc(S["w_turned"], 1)

            pe.wait_ge(S["rows_made"], 1)
            if OVERLAP:
                pe.wait_ge(S["pool_masked"], 2)
            for table in range(4):
                wait_count(pe, S["tables_copied"], table)
                for s in range(2):
                    for j in range(TILES):
                        last = nc.tensor.transpose(banks[:, 6 + s, j * R:(j + 1) * R],
                                                   index_rows[0:R, table, s, j:GROUP:TILES], ident[0:R, 0:R])
                last.then_inc(S["tables_turned"], 1)
            nc.tensor.transpose(banks[0:2, 4, 0:R], base_f[0:R, :], ident[0:R, 0:R])
            nc.tensor.transpose(banks[0:1, 4, P:P + R], span_max[0:R, :], ident[0:R, 0:R]).then_inc(S["base_turned"], 1)

            def turn_x(i, h):
                t = 2 * i + h
                pe.wait_ge(S[f"xa_loaded{h}"], 16 * (i + 1))
                wait_count(pe, S["xa_ready"], t - 1)
                for k in range(KC):
                    last = nc.tensor.transpose(banks[:, h, k * NODES:(k + 1) * NODES],
                                               x_t[:, h, k * P:(k + 1) * P], ident[0:NODES, 0:NODES])
                last.then_inc(S["xa_turned"], 1)

            def product_x(i, h):
                t = 2 * i + h
                pe.wait_ge(S["xa_ready"], t + 1)
                wait_count(pe, S["p_ready"], t - 1)
                for k in range(KC):
                    last = nc.tensor.matmul(banks[0:NODES, 2 + h, :], x_turned_sb[:, h, k, :], w_x[:, k, :],
                                            start=k == 0, stop=k == KC - 1)
                last.then_inc(S["p_product"], 1)

            def count(i, half):
                for k, d in enumerate(count_turns(i, half)):
                    slot = (half * (COUNTS // 2) + k) % 2
                    pe.wait_ge(S["deg_hot"], d + 1)
                    for u in range(STEP):
                        last = nc.tensor.matmul(banks[0:NB, 4, 0:P], hot_hi[:, slot, u, :], hot_lo[:, slot, u, :],
                                                start=isinstance(d, int) and d == 0 and u == 0,
                                                stop=isinstance(d, int) and d == R - 1 and u == STEP - 1,
                                                skip_group_check=True)
                    last.then_inc(S["deg_counted"], 1)

            def node_turn(i):
                for h in range(2):
                    if not isinstance(i, int) or i >= 1:
                        product_x(i - 1, h)
                    turn_x(i, h)
                    count(i, h)

            pe.wait_ge(S["fits_known"], 1)
            over_setup(pe, node_turn, NN // 2)
            for h in range(2):
                product_x(NN // 2 - 1, h)

            pe.wait_ge(S["xa_ready"], NN)
            pe.wait_ge(S["p_ready"], NN)
            pe.wait_ge(S["dinv_made"], 1)
            pe.wait_ge(S["w_copied"], 1)
            pe.wait_ge(S["tables_copied"], 4)
            pe.wait_ge(S["w_split"], 1)

            def turn_ea(turn, s):
                g = 2 * turn + s
                if isinstance(g, int) and not 0 <= g < NG:
                    return
                pe.wait_ge(S["ea_split"], g + 1)
                wait_count(pe, S["ea_ready"], g)
                for j in range(TILES):
                    last = nc.tensor.transpose(banks[:, 7, j * P:(j + 1) * P],
                                               ea_parts[:, j, :, :].rearrange("p a d -> p (a d)").bitcast(F32),
                                               ident[:, :])
                last.then_inc(S["ea_turned"], 1)

            def edge_product(turn, u, t, g):
                if isinstance(t, int) and not 0 <= t < NT:
                    return
                s, j = u // TILES, u % TILES
                if j == 0:
                    pe.wait_ge(S["ea_ready"], 2 * turn + s + 1)
                wait_count(pe, S["pre_ready"], t - 1)
                lhs = ea_turned_sb[:, s, j * P:(j + 1) * P]
                nc.tensor.matmul(banks[:, u % 2, :], lhs, w_e_hi[:, :], start=True, stop=False)
                nc.tensor.matmul(banks[:, u % 2, :], lhs, w_e_lo[:, :], start=False, stop=True).then_inc(
                    S["edge_product"], 1)

            def turn_pre(turn, u, t, g):
                if isinstance(t, int) and not 0 <= t < NT:
                    return
                pe.wait_ge(S["pre_ready"], t + 1)
                wait_count(pe, S["hidden_ready"], t - 1)
                for k in range(KC):
                    last = nc.tensor.transpose(banks[:, 2 + u % 2, k * P:(k + 1) * P],
                                               pre[:, u % 2, k * P:(k + 1) * P], ident[:, :])
                last.then_inc(S["pre_turned"], 1)

            def core_product(turn, u, t, g):
                if isinstance(t, int) and not 0 <= t < NT:
                    return
                pe.wait_ge(S["hidden_ready"], t + 1)
                wait_count(pe, S["msg_ready"], t - 1)
                for k in range(KC):
                    last = nc.tensor.matmul(banks[:, 4 + u % 2, 0:H], hidden[:, u % 2, k, :], w_2[:, k, :],
                                            start=k == 0, stop=k == KC - 1)
                last.then_inc(S["core_done"], 1)

            def scatter(rows_of, ready, hop, turn, u, t, g):
                if isinstance(t, int) and not 0 <= t < NT:
                    return
                j = u % TILES
                ready(turn, u, t, g)
                pe.wait_ge(S[hop + "hot_ready"], t + 1)
                if j == 0:
                    wait_count(pe, S[hop + "agg_added"], g)
                for k in range(KC):
                    last = nc.tensor.matmul(banks[:, 6, k * WINDOW:(k + 1) * WINDOW],
                                            rows_of(u)[:, k * P:(k + 1) * P], hot[:, u % STEP, :],
                                            start=j == 0 and k == 0, stop=j == TILES - 1, skip_group_check=True)
                last.then_inc(S[hop + "scattered"], 1)

            def scatter_anywhere(rows_of, ready, hop, turn, u, t, g):
                if isinstance(t, int) and not 0 <= t < NT:
                    return
                ready(turn, u, t, g)
                if u % TILES < TILES - 1:
                    return
                pe.sem_inc(S["slow_begun"], 1)
                with pe.Fori(0, NB) as w:
                    pe.wait_ge(S[hop + "slow_hot"], g * NB + w + 1)
                    pe.wait_ge(S[hop + "slow_added"], g * NB + w + 1)
                    for jj in range(TILES):
                        uu = u - TILES + 1 + jj
                        for k in range(KC):
                            last = nc.tensor.matmul(banks[:, 6, k * WINDOW:(k + 1) * WINDOW],
                                                    rows_of(uu)[:, k * P:(k + 1) * P], hot[:, uu % STEP, :],
                                                    start=jj == 0 and k == 0, stop=jj == TILES - 1,
                                                    skip_group_check=True)
                    last.then_inc(S[hop + "slow_scattered"], 1)

                pe.wait_ge(S[hop + "slow_added"], (g + 1) * NB + 1)
                for _ in range(TILES):
                    pe.sem_inc(S[hop + "scattered"], 1)

            def msg_of(u):
                return msg[:, u, :]

            def msg_is_ready(turn, u, t, g):
                pe.wait_ge(S["msg_ready"], t + 1)

            def edge_steps(scatter_stage):
                def step(i, u):
                    edge_product(*ahead(i, u, 2))
                    turn_pre(*ahead(i, u, 1))
                    core_product(*ahead(i, u, 0))
                    scatter_stage(msg_of, msg_is_ready, "", *ahead(i, u, -1))
                    if u % TILES == 0:
                        turn, place, _, _ = ahead(i, u, TILES)
                        turn_ea(turn, place // TILES)
                over_tiles(pe, step, -TILES, NT + 1, R)

            in_order = pe.value_load(fits[0:1, 0:1], min_val=0, max_val=1)
            with pe.If(in_order):
                edge_steps(scatter)
            with pe.Else():
                edge_steps(scatter_anywhere)

            def turn_win(t, h):
                pe.wait_ge(S["win_copied"], t + 1)
                wait_count(pe, S["node_summed"], t - 1)
                for k in range(KC):
                    last = nc.tensor.transpose(banks[0:NODES, h, k * P:(k + 1) * P], x_turned_sb[:, h, k, :],
                                               ident[:, :])
                last.then_inc(S["win_turned"], 1)

            def turn_g(t, h):
                pe.wait_ge(S["g_ready"], t + 1)
                wait_count(pe, S["g_back"], t - 1)
                for k in range(KC):
                    last = nc.tensor.transpose(banks[:, 2 + h, k * NODES:(k + 1) * NODES],
                                               g_t[:, h, k * P:(k + 1) * P], ident[0:NODES, 0:NODES])
                last.then_inc(S["g_turned"], 1)

            pe.wait_ge(S["agg_added"], NG)
            def node_step(i, u):
                at_tile(turn_win, i, u, 1)
                at_tile(turn_g, i, u, -3)

            over_nodes(pe, node_step, -1, NN + 3)

            def hop_steps(k, scatter_stage):
                def rows_of(u):
                    return hop_rows[:, u // TILES, u % TILES, :]

                def are_gathered(turn, u, t, g):
                    if u % TILES == 0:
                        pe.wait_ge(S[f"h{k}_gathered{u // TILES}"], 16 * TILES * (turn + 1))

                def step(i, u):
                    scatter_stage(rows_of, are_gathered, f"h{k}_", *ahead(i, u, 0, HOP_STEP))
                over_tiles(pe, step, 0, NT, HR, HOP_STEP)

            for k in range(2):
                with pe.If(in_order):
                    hop_steps(k, scatter)
                with pe.Else():
                    hop_steps(k, scatter_anywhere)
                if k == 0:
                    def turn_hop(t, h):
                        pe.wait_ge(S["win_copied"], NN + t + 1)
                        wait_count(pe, S["hop_ready"], t - 1)
                        for c in range(KC):
                            last = nc.tensor.transpose(banks[0:NODES, h, c * P:(c + 1) * P], x_turned_sb[:, h, c, :],
                                                       ident[:, :])
                        last.then_inc(S["hop_turned"], 1)

                    for h in range(2):
                        turn_hop(h, h)
                    with pe.Fori(1, NN // 2) as i:
                        for h in range(2):
                            turn_hop(2 * i + h, h)

            def logits(t, h):
                pe.wait_ge(S["win_copied"], 2 * NN + t + 1)
                wait_count(pe, S["logit_rows"], t - 1)
                for k in range(KC):
                    last = nc.tensor.matmul(banks[0:NODES, h, 0:H], x_turned_sb[:, h, k, :], w_l_turned[:, k, :],
                                            start=k == 0, stop=k == KC - 1)
                last.then_inc(S["logits_done"], 1)

            for h in range(2):
                logits(h, h)
            with pe.Fori(1, NN // 2) as i:
                for h in range(2):
                    logits(2 * i + h, h)

        @block.scalar
        def _(act):
            def copy_x(i, h):
                t = 2 * i + h
                act.wait_ge(S["xa_turned"], t + 1)
                wait_count(act, S["p_product"], t - 1)
                nc.scalar.copy(x_turned_sb[:, h, :, :].rearrange("p k n -> p (k n)"),
                               banks[:, h, 0:KC * NODES]).then_inc(S["xa_ready"], 1)

            def store_p(i, h):
                t = 2 * i + h
                act.wait_ge(S["p_ready"], t + 1)
                act.dma_start(node_rows(p_table, t), p_t[:, h, :]).then_inc(S[f"p_stored{h}"], 16)

            def node_turn(i):
                for h in range(2):
                    copy_x(i, h)
                    if not isinstance(i, int) or i >= 1:
                        store_p(i - 1, h)

            over_setup(act, node_turn, NN // 2)
            for h in range(2):
                store_p(NN // 2 - 1, h)

            act.wait_ge(S["deg_made"], 1)
            nc.scalar.activation(dinv_rows[:, :], dinv_rows[:, :], ACT.Sqrt).then_inc(S["deg_rooted"], 1)

            def copy_index(index, gathered, slots, turn, s):
                if isinstance(turn, int) and turn >= NG // slots:
                    return
                wait_count(act, S[f"{gathered}{s}"], 16 * TILES * turn)
                c = TILES * (slots * turn + s)
                columns = src_t[:, c:c + TILES] if isinstance(c, int) else src_t[:, ds(c, TILES)]
                nc.scalar.copy(index_now[:, s, :], columns).then_inc(S[index], 1)

            def copy_ea(turn, s):
                g = 2 * turn + s
                if isinstance(g, int) and not 0 <= g < NG:
                    return
                act.wait_ge(S["ea_turned"], g + 1)
                wait_count(act, S["edge_product"], TILES * (g - 1))
                nc.scalar.copy(ea_turned_sb[:, s, :], banks[:, 7, :]).then_inc(S["ea_ready"], 1)

            def activate(turn, u, t, g):
                if isinstance(t, int) and not 0 <= t < NT:
                    return
                act.wait_ge(S["pre_ready"], t + 1)
                wait_count(act, S["msg_ready"], t - 1)
                nc.scalar.activation(gate[:, u % 2, :], pre[:, u % 2, H:H2], ACT.Sigmoid).then_inc(S["gate_ready"], 1)
                act.wait_ge(S["pre_turned"], t + 1)
                wait_count(act, S["core_done"], t - 1)
                nc.scalar.activation(hidden[:, u % 2, :, :].rearrange("p k n -> p (k n)"), banks[:, 2 + u % 2, 0:H],
                                     ACT.Relu).then_inc(S["hidden_ready"], 1)

            def step(i, u):
                activate(*ahead(i, u, 1))
                if u % TILES == 0:
                    turn, place, _, _ = ahead(i, u, TILES)
                    copy_ea(turn, place // TILES)
                    if not (isinstance(i, int) and i < 0):
                        copy_index("p_index", "p_gathered", 2, i + 1, u // TILES)

            act.wait_ge(S["tables_copied"], 4)
            for s in range(2):
                copy_index("p_index", "p_gathered", 2, 0, s)
            over_tiles(act, step, -TILES, NT, R)

            def copy_win(turned):
                def stage(t, h):
                    wait_count(act, S[turned], t - 1)
                    if turned == "hop_turned":
                        act.wait_ge(S["hop_scaled"], t + 1)
                    nc.scalar.copy(x_turned_sb[:, h, :, :], node_cols(agg, t)).then_inc(S["win_copied"], 1)
                return stage

            def deviation(n, norm):
                def stage(t, h):
                    act.wait_ge(S[norm + "_moments"], t + 1)
                    nc.scalar.activation(scale[:, n, h:h + 1], moments[:, n, h, 1:2], ACT.Sqrt, bias=eps[:, :]).then_inc(
                        S[norm + "_deviation"], 1)
                return stage

            def normalise(n, rows, result, h):
                return nc.scalar.activation(result, rows, ACT.Identity, scale=scale[:, n, h:h + 1],
                                            bias=shift[:, n, h:h + 1])

            def first_norm(t, h):
                act.wait_ge(S["node_shift"], t + 1)
                normalise(0, node[:, h, :], node[:, h, :], h).then_inc(S["node_normed"], 1)

            def second_norm(t, h):
                act.wait_ge(S["sum_shift"], t + 1)
                normalise(1, sum_t[:, h, :], x3_rows(t), h).then_inc(S["x3_ready"], 1)

            def scale_g(t, h):
                act.wait_ge(S["x3_ready"], t + 1)
                wait_count(act, S["g_turned"], t - 1)
                wait_count(act, S[f"g_stored{h}"], 8 * (t - h))
                nc.scalar.activation(g_t[:, h, :], x3_rows(t), ACT.Copy, scale=column(dinv_col, t)).then_inc(
                    S["g_ready"], 1)

            def back_g(t, h):
                act.wait_ge(S["g_turned"], t + 1)
                nc.scalar.copy(node_cols(agg, t), banks[:, 2 + h, 0:KC * NODES].rearrange("p (k n) -> p k n", k=KC)
                               ).then_inc(S["g_back"], 1)

            def node_step(i, u):
                at_tile(deviation(1, "sum"), i, u, -3)
                at_tile(first_norm, i, u, -1)
                at_tile(copy_win("win_turned"), i, u, 1)
                at_tile(back_g, i, u, -4)
                at_tile(second_norm, i, u, -3)
                at_tile(deviation(0, "node"), i, u, 0)
                at_tile(scale_g, i, u, -3)

            act.wait_ge(S["agg_added"], NG)
            act.wait_ge(S["dinv_loaded"], 32)
            act.wait_ge(S["consts_ready"], 2)
            over_nodes(act, node_step, -1, NN + 4)

            for s in range(HOP_SLOTS):
                copy_index("h0_index", "h0_gathered", HOP_SLOTS, 0, s)
            with act.Fori(1, HR) as i:
                for s in range(HOP_SLOTS):
                    copy_index("h0_index", "h0_gathered", HOP_SLOTS, i, s)

            def copy_hop(t, h):
                act.wait_ge(S["hop_turned"], t + 1)
                wait_count(act, S[f"hop_stored{h}"], 8 * (t - h))
                nc.scalar.copy(g_t[:, h, :], banks[0:NODES, h, 0:H]).then_inc(S["hop_ready"], 1)

            for h in range(2):
                act.wait_ge(S[f"g_stored{h}"], 8 * NN)
            def hop_step(i, u):
                at_tile(copy_win("hop_turned"), i, u, 1)
                at_tile(copy_hop, i, u, 0)

            over_nodes(act, hop_step, -1, NN)

            for s in range(HOP_SLOTS):
                copy_index("h1_index", "h1_gathered", HOP_SLOTS, 0, s)
            with act.Fori(1, HR) as i:
                for s in range(HOP_SLOTS):
                    copy_index("h1_index", "h1_gathered", HOP_SLOTS, i, s)

            def exponentials(t, h):
                act.wait_ge(S["l_chain"], t + 1)
                wait_count(act, S["expd"], t - 1)
                nc.scalar.activation(expo[:, h, :], node[:, h, :], ACT.Exp, bias=top[:, h, 1:2],
                                     accum_out=column(sums, t)).then_inc(S["expd"], 1)

            def logit_step(i, u):
                at_tile(copy_win("logits_done"), i, u, 1)
                at_tile(exponentials, i, u, 0)

            act.wait_ge(S["h1_agg_added"], NG)
            over_nodes(act, logit_step, -1, NN)
            act.wait_ge(S["expd"], NN)
            nc.scalar.activation(lse[:, :], sums[:, :], ACT.Ln).then_inc(S["lse_ready"], 1)

            def last_norm(t, h):
                act.wait_ge(S["y_shift"], t + 1)
                wait_count(act, S[f"y_stored{h}"], 8 * (t - h))
                normalise(0, node[:, h, :], y_t[:, h, :], h).then_inc(S["y_ready"], 1)

            def last_step(i, u):
                at_tile(last_norm, i, u, -1)
                at_tile(deviation(0, "y"), i, u, 0)

            over_nodes(act, last_step, 0, NN + 1)

        @block.vector
        def _(dve):
            done = [0]

            def then(instruction):
                done[0] += 1
                instruction.then_inc(S["self_dve"], 1)
                dve.wait_ge(S["self_dve"], done[0])

            dve.wait_ge(S["setup_loaded"], 16 * setup_dmas[0])
            nc.vector.tensor_copy(dst_f[0:R, :, :], dst_rows[0:R, :, :])
            nc.vector.tensor_copy(index_rows[0:R, 0, :, :], src_rows[0:R, :, :])
            nc.vector.tensor_single_scalar(hi_i[0:R, :, :], dst_rows[0:R, :, :], WINDOW.bit_length() - 1,
                                           ALU.arith_shift_right)
            then(nc.vector.tensor_single_scalar(lo_i[0:R, :, :], dst_rows[0:R, :, :], WINDOW - 1, ALU.bitwise_and))
            nc.vector.tensor_copy(index_rows[0:R, 2, :, :], hi_i[0:R, :, :])
            nc.vector.tensor_copy(index_rows[0:R, 3, :, :], lo_i[0:R, :, :])
            nc.vector.tensor_reduce(base_f[0:R, :], dst_f[0:R, :, :], AX.X, ALU.min)
            then(nc.vector.tensor_reduce(top_f[0:R, :], dst_f[0:R, :, :], AX.X, ALU.max))
            then(nc.vector.tensor_tensor(span_f[0:R, :], top_f[0:R, :], base_f[0:R, :], ALU.subtract))
            then(nc.vector.tensor_reduce(span_max[0:R, :], span_f[0:R, :], AX.X, ALU.max))
            nc.vector.tensor_tensor(index_rows[0:R, 1, :, :], dst_f[0:R, :, :],
                                    base_f[0:R, :].unsqueeze(2).to_broadcast([R, 2, GROUP]),
                                    ALU.subtract).then_inc(S["rows_made"], 1)
            dve.wait_ge(S["iota_made"], 3)
            nc.vector.tensor_copy(block_starts[:, :], block_i[:, :])
            nc.vector.tensor_copy(iota[:, :], iota_i[:, :])
            nc.vector.tensor_copy(iota_b[:, :], iota_i[:, :])
            then(nc.vector.tensor_copy(w_e_hi[:, :], w_e[:, :]))
            nc.vector.tensor_tensor(w_e_lo[:, :], w_e[:, :], w_e_hi[:, :].bitcast(F32), ALU.subtract).then_inc(
                S["w_split"], 1)
            dve.wait_ge(S["w_turned"], 1)
            nc.vector.tensor_copy(w_l_turned[:, :, :].rearrange("p k n -> p (k n)"), banks[:, 5, :]).then_inc(
                S["w_copied"], 1)
            for n, table in enumerate((src_t, local_t, hi_t, lo_t)):
                dve.wait_ge(S["tables_turned"], n + 1)
                by_tile = table[:, :].rearrange("p (i s j) -> p i s j", s=2, j=TILES)
                for s in range(2):
                    last = nc.vector.tensor_copy(by_tile[:, :, s, :],
                                                 banks[:, 6 + s, 0:TILES * R].rearrange("p (j i) -> p i j", j=TILES))
                last.then_inc(S["tables_copied"], 1)
            dve.wait_ge(S["tables_copied"], 4)
            dve.wait_ge(S["base_turned"], 1)
            nc.vector.tensor_copy(bases[:, :], banks[0:2, 4, 0:R])
            then(nc.vector.tensor_reduce(widest[:, :], banks[0:1, 4, P:P + R], AX.X, ALU.max))
            nc.vector.tensor_single_scalar(fits[:, :], widest[:, :], float(WINDOW), ALU.is_lt).then_inc(S["fits_known"], 1)

            def bias_p(i, h):
                t = 2 * i + h
                dve.wait_ge(S["p_product"], t + 1)
                wait_count(dve, S[f"p_stored{h}"], 8 * (t - h))
                nc.vector.tensor_tensor(p_t[:, h, :], banks[0:NODES, 2 + h, :], bias_in[0:NODES, :],
                                        ALU.add).then_inc(S["p_ready"], 1)

            def node_turn(i):
                for half in range(2):
                    for k, d in enumerate(count_turns(i, half)):
                        wait_count(dve, S["deg_counted"], d - 1)
                        slot = (half * (COUNTS // 2) + k) % 2
                        nc.vector.tensor_tensor(
                            hot_hi[:, slot, :, :], iota_b[:, 0:NB].unsqueeze(1).to_broadcast([P, STEP, NB]),
                            tile_columns(hi_t, d).unsqueeze(2).to_broadcast([P, STEP, NB]), ALU.is_equal)
                        nc.vector.tensor_tensor(
                            hot_lo[:, slot, :, :], iota_b[:, :].unsqueeze(1).to_broadcast([P, STEP, P]),
                            tile_columns(lo_t, d).unsqueeze(2).to_broadcast([P, STEP, P]),
                            ALU.is_equal).then_inc(S["deg_hot"], 1)
                    if not isinstance(i, int) or i >= 1:
                        bias_p(i - 1, half)

            over_setup(dve, node_turn, NN // 2)
            for h in range(2):
                bias_p(NN // 2 - 1, h)
            dve.wait_ge(S["deg_counted"], R)
            nc.vector.tensor_single_scalar(dinv_rows[:, :], banks[0:NB, 4, 0:P], 1.0, ALU.add).then_inc(
                S["deg_made"], 1)

            dst_t = hi_t
            then(nc.vector.scalar_tensor_tensor(out=dst_t[:, :], in0=hi_t[:, :], scalar=float(WINDOW), in1=lo_t[:, :],
                                                op0=ALU.mult, op1=ALU.add))

            dve.wait_ge(S["deg_rooted"], 1)
            nc.vector.reciprocal(dinv_rows[:, :], dinv_rows[:, :]).then_inc(S["dinv_made"], 1)

            def split_ea(turn, s):
                g = 2 * turn + s
                if isinstance(g, int) and not 0 <= g < NG:
                    return
                dve.wait_ge(S[f"ea_loaded{s}"], 16 * (turn + 1))
                wait_count(dve, S["ea_turned"], g)
                nc.vector.tensor_copy(ea_parts[:, :, 0, :], ea[:, s, :, :]).then_inc(S["ea_rounded"], 1)
                dve.wait_ge(S["ea_rounded"], g + 1)
                nc.vector.tensor_tensor(ea_parts[:, :, 1, :], ea[:, s, :, :], ea_parts[:, :, 0, :].bitcast(F32),
                                        ALU.subtract).then_inc(S["ea_split"], 1)

            def add_product(turn, u, t, g):
                if isinstance(t, int) and not 0 <= t < NT:
                    return
                s, j = u // TILES, u % TILES
                dve.wait_ge(S["edge_product"], t + 1)
                if j == 0:
                    dve.wait_ge(S[f"p_gathered{s}"], 16 * TILES * (turn + 1))
                wait_count(dve, S["pre_turned"], t - 1)
                wait_count(dve, S["gate_ready"], t - 1)
                nc.vector.tensor_tensor(pre[:, u % 2, :], banks[:, u % 2, :], gathered[:, s, j, :],
                                        ALU.add).then_inc(S["pre_ready"], 1)

            def message(turn, u, t, g):
                if isinstance(t, int) and not 0 <= t < NT:
                    return
                dve.wait_ge(S["core_done"], t + 1)
                wait_count(dve, S["msg_ready"], t)
                nc.vector.tensor_tensor(core[:, :], banks[:, 4 + u % 2, 0:H], bias_core[:, :], ALU.add).then_inc(
                    S["core_biased"], 1)
                dve.wait_ge(S["core_biased"], t + 1)
                dve.wait_ge(S["gate_ready"], t + 1)
                wait_count(dve, S["scattered"], t - STEP + 1)
                nc.vector.tensor_tensor(msg[:, u, :], core[:, :], gate[:, u % 2, :], ALU.mult).then_inc(
                    S["msg_ready"], 1)

            def one_hot(hop, turn, u, t, g):
                if isinstance(t, int) and not 0 <= t < NT:
                    return
                wait_count(dve, S[hop + "scattered"], t - STEP + 1)
                nc.vector.tensor_single_scalar(hot[:, u % STEP, :], iota[:, 0:WINDOW], column(local_t, t),
                                               ALU.is_equal).then_inc(S[hop + "hot_ready"], 1)

            def add_window(hop, turn, u, t, g):
                if isinstance(t, int) and not 0 <= t < NT:
                    return
                if u % TILES < TILES - 1:
                    return
                s, pair_of = u // TILES % 2, (STEP if hop == "" else HOP_STEP) // STEP * turn + u // STEP
                at = bases[s:s + 1, pair_of:pair_of + 1] if isinstance(turn, int) else bases[s:s + 1, ds(pair_of, 1)]
                base = dve.value_load(at, min_val=0, max_val=N - 1)
                dve.wait_ge(S[hop + "scattered"], TILES * (g + 1))
                wait_count(dve, S[hop + "agg_added"], g)
                where = agg[:, :, ds(base, WINDOW)]
                nc.vector.tensor_tensor(where, where, banks[:, 6, 0:KC * WINDOW].rearrange("p (k n) -> p k n", k=KC),
                                        ALU.add).then_inc(S[hop + "agg_added"], 1)

            def no_one_hot(hop, turn, u, t, g):
                pass

            def add_anywhere(hop, turn, u, t, g):
                if isinstance(t, int) and not 0 <= t < NT:
                    return
                j = u % TILES
                if j < TILES - 1:
                    return
                with dve.Fori(0, NB) as w:
                    dve.wait_ge(S[hop + "slow_added"], g * NB + w + 1)
                    for jj in range(TILES):
                        last = nc.vector.tensor_scalar(hot[:, (u - j + jj) % STEP, :], iota[:, 0:WINDOW],
                                                       column(dst_t, t - j + jj), block_starts[:, ds(w, 1)],
                                                       ALU.subtract, ALU.is_equal)
                    last.then_inc(S[hop + "slow_hot"], 1)
                    dve.wait_ge(S[hop + "slow_scattered"], g * NB + w + 1)
                    where = agg[:, :, ds(WINDOW * w, WINDOW)]
                    nc.vector.tensor_tensor(where, where,
                                            banks[:, 6, 0:KC * WINDOW].rearrange("p (k n) -> p k n", k=KC),
                                            ALU.add).then_inc(S[hop + "slow_added"], 1)
                dve.wait_ge(S[hop + "slow_added"], (g + 1) * NB + 1)
                dve.sem_inc(S[hop + "agg_added"], 1)

            def edge_steps(hot_stage, add_stage):
                def step(i, u):
                    hot_stage("", *ahead(i, u, 0))
                    add_product(*ahead(i, u, 2))
                    message(*ahead(i, u, 0))
                    add_stage("", *ahead(i, u, -1))
                    if u % TILES == 2:
                        turn, place, _, _ = ahead(i, u, TILES + 2)
                        split_ea(turn, place // TILES)
                over_tiles(dve, step, -TILES - 2, NT + 1, R)

            def hop_steps(hop, hot_stage, add_stage):
                def step(i, u):
                    if u % TILES == 0:
                        for j in range(TILES):
                            hot_stage(hop, *ahead(i, u, TILES + j, HOP_STEP))
                    add_stage(hop, *ahead(i, u, 0, HOP_STEP))
                over_tiles(dve, step, -TILES, NT, HR, HOP_STEP)

            in_order = dve.value_load(fits[0:1, 0:1], min_val=0, max_val=1)
            dve.wait_ge(S["agg_cleared"], 1)
            with dve.If(in_order):
                edge_steps(one_hot, add_window)
            with dve.Else():
                dve.sem_inc(S["slow_added"], 1)
                edge_steps(no_one_hot, add_anywhere)

            def reciprocal(n, norm):
                def stage(t, h):
                    dve.wait_ge(S[norm + "_deviation"], t + 1)
                    nc.vector.reciprocal(scale[:, n, h:h + 1], scale[:, n, h:h + 1]).then_inc(S[norm + "_scale"], 1)
                return stage

            def less_mean(n, norm):
                def stage(t, h):
                    dve.wait_ge(S[norm + "_scale"], t + 1)
                    nc.vector.scalar_tensor_tensor(out=shift[:, n, h:h + 1], in0=moments[:, n, h, 0:1], scalar=-1.0,
                                                   in1=scale[:, n, h:h + 1], op0=ALU.mult, op1=ALU.mult).then_inc(
                        S[norm + "_shift"], 1)
                return stage

            def statistics(n, norm, rows, summed):
                def stage(t, h):
                    dve.wait_ge(S[summed], t + 1)
                    nc.vector.bn_stats(stats[:, n, h, :], rows[:, h, :]).then_inc(S[norm + "_stats"], 1)
                return stage

            def put_together(n, norm):
                def stage(t, h):
                    dve.wait_ge(S[norm + "_stats"], t + 1)
                    dve.sem_inc(S["begun"], 1)
                    nc.vector.bn_aggr(moments[:, n, h, :], stats[:, n, h, :]).then_inc(S[norm + "_moments"], 1)
                return stage

            def first_sum(t, h):
                dve.wait_ge(S["win_turned"], t + 1)
                wait_count(dve, S["sum_ready"], t - 1)
                nc.vector.tensor_tensor(node[:, h, :], banks[0:NODES, h, 0:H], x3_rows(t), ALU.add).then_inc(
                    S["node_summed"], 1)

            def second_sum(t, h):
                dve.wait_ge(S["beta_added"], t + 1)
                dve.wait_ge(S["gamma_scaled"], t + 1)
                wait_count(dve, S["x3_ready"], t - 1)
                nc.vector.tensor_tensor(sum_t[:, h, :], node[:, h, :], x3_rows(t), ALU.add).then_inc(S["sum_ready"], 1)

            def node_step(i, u):
                at_tile(reciprocal(0, "node"), i, u, -1)
                at_tile(second_sum, i, u, -2)
                at_tile(less_mean(0, "node"), i, u, -1)
                at_tile(first_sum, i, u, 0)
                at_tile(reciprocal(1, "sum"), i, u, -3)
                at_tile(statistics(1, "sum", sum_t, "sum_ready"), i, u, -2)
                at_tile(less_mean(1, "sum"), i, u, -3)
                at_tile(statistics(0, "node", node, "node_summed"), i, u, 0)
                at_tile(put_together(1, "sum"), i, u, -2)
                at_tile(put_together(0, "node"), i, u, 0)

            dve.wait_ge(S["x_loaded"], 5 * 16)
            over_nodes(dve, node_step, 0, NN + 3)

            dve.wait_ge(S["dinv_loaded"], 32)
            nc.vector.tensor_tensor(dinv_all[:, :], dinv_all[:, :], dinv_all[:, :], ALU.mult).then_inc(
                S["dinv_squared"], 1)
            dve.wait_ge(S["g_back"], NN)
            for k in range(2):
                hop = f"h{k}_"
                with dve.If(in_order):
                    hop_steps(hop, one_hot, add_window)
                with dve.Else():
                    dve.sem_inc(S[hop + "slow_added"], 1)
                    hop_steps(hop, no_one_hot, add_anywhere)
                if k == 0:
                    def scale_hop(t, h):
                        where = node_cols(agg, t)
                        cols = (dinv_all[:, NODES * t:NODES * (t + 1)] if isinstance(t, int)
                                else dinv_all[:, ds(NODES * t, NODES)])
                        nc.vector.tensor_tensor(where, where, cols.unsqueeze(1).to_broadcast([P, KC, NODES]),
                                                ALU.mult).then_inc(S["hop_scaled"], 1)

                    dve.wait_ge(S["h0_agg_added"], NG)
                    dve.wait_ge(S["dinv_squared"], 1)
                    over_nodes(dve, lambda i, u: at_tile(scale_hop, i, u, 0), 0, NN)
                    dve.wait_ge(S["win_copied"], 2 * NN)

            def logit_rows(t, h):
                dve.wait_ge(S["logits_done"], t + 1)
                wait_count(dve, S["expd"], t - 1)
                wait_count(dve, S["y_added"], t - 1)
                nc.vector.scalar_tensor_tensor(out=node[:, h, :], in0=banks[0:NODES, h, 0:H],
                                               scalar=column(dinv_col, t), in1=bias_l[0:NODES, :], op0=ALU.mult,
                                               op1=ALU.add).then_inc(S["logit_rows"], 1)

            def logit_top(t, h):
                dve.wait_ge(S["logit_rows"], t + 1)
                nc.vector.tensor_reduce(top[:, h, 0:1], node[:, h, :], AX.X, ALU.max).then_inc(S["logit_top"], 1)
                dve.wait_ge(S["logit_top"], t + 1)
                nc.vector.tensor_single_scalar(top[:, h, 1:2], top[:, h, 0:1], -1.0, ALU.mult).then_inc(S["l_chain"], 1)

            def add_logits(t, h):
                dve.wait_ge(S["l_chain"], t + 1)
                nc.vector.scalar_tensor_tensor(out=x3_rows(t), in0=node[:, h, :], scalar=top[:, h, 1:2], in1=x3_rows(t),
                                               op0=ALU.add, op1=ALU.add).then_inc(S["y_added"], 1)

            def logit_step(i, u):
                at_tile(logit_rows, i, u, 0)
                at_tile(add_logits, i, u, -1)
                at_tile(logit_top, i, u, 0)

            over_nodes(dve, logit_step, 0, NN + 1)

            def last_sum(t, h):
                wait_count(dve, S["y_ready"], t - 1)
                nc.vector.tensor_scalar(node[:, h, :], x3_rows(t), column(lse, t), None, ALU.subtract).then_inc(
                    S["y_summed"], 1)

            def last_step(i, u):
                at_tile(last_sum, i, u, 0)
                at_tile(reciprocal(0, "y"), i, u, -1)
                at_tile(statistics(0, "y", node, "y_summed"), i, u, 0)
                at_tile(less_mean(0, "y"), i, u, -1)
                at_tile(put_together(0, "y"), i, u, 0)

            dve.wait_ge(S["lse_ready"], 1)
            dve.wait_ge(S["y_added"], NN)
            over_nodes(dve, last_step, 0, NN + 1)


_INS = ["x", "src", "dst", "edge_attr_64", "L0_gnn_W1", "L0_gnn_b1", "L0_gnn_W2", "L0_gnn_b2", "L0_gnn_Wg",
        "L0_gnn_bg", "L0_gnn_gamma", "L0_gnn_beta", "L1_gnn_W", "L1_gnn_b"]


def kernel(**inputs):
    import concourse.bacc as bacc
    from concourse.bass_utils import run_bass_kernel_spmd

    nc = bacc.Bacc("TRN2", target_bir_lowering=False, num_devices=1)
    arrays, args = {}, []
    for name in _INS:
        a = np.ascontiguousarray(inputs[name])
        arrays[f"in_{name}"] = a
        args.append(nc.dram_tensor(f"in_{name}", a.shape, mybir.dt.from_np(a.dtype), kind="ExternalInput").ap())
    out = nc.dram_tensor("out", inputs["x"].shape, F32, kind="ExternalOutput").ap()
    gnn_kernel(nc, *args, out)
    result = run_bass_kernel_spmd(nc, [arrays], core_ids=[0])
    return result.results[0]["out"]
```

```python
from contextlib import ExitStack

import numpy as np

import concourse.bass as bass
import concourse.mybir as mybir

P = 128
GROUP = 512
TILES = 4
WINDOW = 128
NODES = 125
STEP = 2 * TILES
HOP_SLOTS = 4
HOP_STEP = HOP_SLOTS * TILES
EPS = 1e-5

F32 = mybir.dt.float32
F32R = mybir.dt.float32r
BF16 = mybir.dt.bfloat16
I32 = mybir.dt.int32
ALU = mybir.AluOpType
ACT = mybir.ActivationFunctionType
AX = mybir.AxisListType
ds = bass.ds


def wait_count(engine, semaphore, count):
    if not isinstance(count, int) or count > 0:
        engine.wait_ge(semaphore, count)


def over_tiles(engine, step, first, last, turns, per=STEP):
    for t in range(first, per):
        step(t // per, t % per)
    with engine.Fori(1, turns - 1) as i:
        for u in range(per):
            step(i, u)
    for t in range(per * (turns - 1), last):
        step(t // per, t % per)


def over_setup(engine, step, turns):
    step(0)
    step(1)
    with engine.Fori(2, turns - 1) as i:
        step(i)
    step(turns - 1)


def ahead(i, u, lag, per=STEP):
    turn, place = i + (u + lag) // per, (u + lag) % per
    return turn, place, per * turn + place, per // TILES * turn + place // TILES


def gnn_kernel(nc, x, src, dst, edge_attr, W1, b1, W2, b2, Wg, bg, gamma, beta, Wl, bl, out):
    N, H = x.shape
    E, DE = edge_attr.shape
    KC = H // P
    H2 = 2 * H
    NG = -(-E // GROUP)
    R = NG // 2
    HR = NG // HOP_SLOTS
    NT = NG * TILES
    OVERLAP = NG * GROUP - E
    NN = N // NODES
    NB = -(-N // WINDOW)
    COUNTS = -(-R // (NN // 2))
    NCOL = N + WINDOW
    assert KC * P == H and 2 * DE == P and NG % HOP_SLOTS == 0 and R <= P and OVERLAP < GROUP
    assert NN * NODES == N and NN % 2 == 0 and NB <= P and H2 == 512 and HR > 2
    PART = 5
    assert NN % (2 * PART) == 0 and 2 * PART * H <= 2 * TILES * H2
    assert COUNTS % 2 == 0 and STEP * P == 2 * 2 * H and 0 <= R - COUNTS * (NN // 2 - 1) <= COUNTS

    p_table = nc.dram_tensor("p_table", (N, H2), F32, kind="Internal").ap()
    hop_table = [nc.dram_tensor(f"hop_table{k}", (N, H), F32, kind="Internal").ap() for k in range(2)]
    dinv_flat = nc.dram_tensor("dinv_flat", (NB * P,), F32, kind="Internal").ap()

    with ExitStack() as ctx:
        def sb(name, shape, dt=F32):
            return ctx.enter_context(nc.sbuf_tensor(name, shape, dt))

        def sem(name):
            return ctx.enter_context(nc.semaphore(name))

        banks = ctx.enter_context(nc.psum_tensor("banks", [P, 8, 512], F32))

        w_e_hi = sb("w_e_hi", [P, H2], F32R)
        w_e_lo = sb("w_e_lo", [P, H2], F32R)
        w_2_hi = sb("w_2_hi", [P, KC, H], F32R)
        w_2_lo = sb("w_2_lo", [P, KC, H], F32R)
        w_l_turned = sb("w_l_turned", [P, KC, H])
        bias_in = sb("bias_in", [P, H2])
        bias_core = sb("bias_core", [P, H])
        gamma_all = sb("gamma_all", [P, H])
        beta_all = sb("beta_all", [P, H])
        bias_l = sb("bias_l", [P, H])
        ident = sb("ident", [P, P])
        iota = sb("iota", [P, P])
        block_starts = sb("block_starts", [P, NB])

        pair = 2 * GROUP
        x3_room = sb("x3_room", [P, max(NN * H, 9 * pair)])
        x3 = x3_room[0:NODES, 0:NN * H].rearrange("p (t n) -> p t n", n=H)

        def rows_at(k, dt):
            return x3_room[:, k * pair:(k + 1) * pair].bitcast(dt).rearrange("p (s e) -> p s e", s=2)

        index_rows = x3_room[:, 0:4 * pair].rearrange("p (k s e) -> p k s e", k=4, s=2)
        dst_f = rows_at(4, F32)
        dst_rows, src_rows, hi_i, lo_i = (rows_at(k, I32) for k in range(5, 9))
        base_f = sb("base_f", [P, 2])
        top_f = sb("top_f", [P, 2])
        span_f = sb("span_f", [P, 2])
        span_max = sb("span_max", [P, 1])
        widest = sb("widest", [1, 1])
        fits = sb("fits", [1, 1], I32)
        bases = sb("bases", [2, R], I32)
        src_t = sb("src_t", [P, NT], I32)
        local_t = sb("local_t", [P, NT])
        hi_t = sb("hi_t", [P, NT])
        lo_t = sb("lo_t", [P, NT])

        agg = sb("agg", [P, KC, NCOL])
        dinv_all = sb("dinv_all", [P, N])
        dinv_col = sb("dinv_col", [NODES, NN])
        dinv_rows = sb("dinv_rows", [max(NB, NN), P])

        hot = sb("hot", [P, STEP, WINDOW])
        gate = sb("gate", [P, TILES, H])
        core = sb("core", [P, 2, H])
        gathered = sb("gathered", [P, 2, TILES, H2])
        start_room = gathered[:, :, :, :].rearrange("p s j n -> p (s j n)")
        w_e = start_room[:, 0:H2]
        w_l = start_room[:, H2:H2 + KC * H].rearrange("p (k n) -> p k n", k=KC)
        iota_i = start_room[:, 2 * H2:2 * H2 + P].bitcast(I32)
        block_i = start_room[:, 2 * H2 + P:2 * H2 + P + NB].bitcast(I32)
        w_2 = start_room[:, 2 * H2 + 2 * P:3 * H2 + 2 * P].rearrange("p (k n) -> p k n", k=KC)
        x_t = start_room[0:NODES, 3 * H2 + 2 * P:4 * H2 + 2 * P].rearrange("p (h n) -> p h n", h=2)
        hots = start_room[:, 4 * H2 + 2 * P:].bitcast(BF16)
        hot_lo = [rows.rearrange("p (u n) -> p u n", u=STEP) for rows in (
            *(hots[:, d * STEP * P:(d + 1) * STEP * P] for d in range(COUNTS - 1)),
            core[:, :, :].rearrange("p j n -> p (j n)").bitcast(BF16))]
        hot_hi = gate[:, :, :].rearrange("p j n -> p (j n)").bitcast(BF16)[:, 0:COUNTS * STEP * NB].rearrange(
            "p (d u n) -> p d u n", d=COUNTS, u=STEP)
        iota_b = hots[:, (COUNTS - 1) * STEP * P:(COUNTS - 1) * STEP * P + P]
        hop_rows = gathered[:, :, :, :].rearrange("p s j n -> p (s j n)").rearrange(
            "p (s j n) -> p s j n", s=HOP_SLOTS, j=TILES)
        hop_out = start_room[0:NODES, 0:2 * PART * H].rearrange("p (t n) -> p t n", n=H)
        index_now = sb("index_now", [P, HOP_SLOTS, TILES], I32)
        ea = sb("ea", [P, 2, TILES, DE])
        ea_turned_sb = sb("ea_turned_sb", [P, 2, GROUP], F32R)
        hidden_hi = sb("hidden_hi", [P, KC, GROUP], F32R)
        hidden_lo = sb("hidden_lo", [P, KC, GROUP], F32R)
        room = sb("room", [P, STEP * H])
        w_x = room[:, 0:KC * H2].rearrange("p (k n) -> p k n", k=KC)
        p_t = room[0:NODES, KC * H2:KC * H2 + 2 * H2].rearrange("p (h n) -> p h n", h=2)
        msg = room[:, :].rearrange("p (u n) -> p u n", u=STEP)
        node, sum_t, g_t, expo = (room[0:NODES, k * 2 * H:(k + 1) * 2 * H].rearrange("p (h n) -> p h n", h=2)
                                  for k in range(4))
        logit_rows_t, y_t = (room[0:NODES, k * 4 * H:(k + 1) * 4 * H].rearrange("p (h n) -> p h n", h=4)
                             for k in range(2))
        x_turned_sb = sb("x_turned_sb", [P, 2, KC, NODES])
        stats = sb("stats", [NODES, 2, 2, 6])
        moments = sb("moments", [NODES, 2, 2, 2])
        last_stats = sb("last_stats", [NODES, 4, 6])
        last_moments_t = sb("last_moments", [NODES, 4, 2])
        last_scale = sb("last_scale", [NODES, 4])
        last_shift = sb("last_shift", [NODES, 4])
        scale = sb("scale", [NODES, 2, 2])
        shift = sb("shift", [NODES, 2, 2])
        eps = sb("eps", [NODES, 1])
        top = sb("top", [NODES, 4, 2])
        sums = sb("sums", [NODES, NN])
        lse = sb("lse", [NODES, NN])

        names = """rows_loaded setup_loaded consts_ready iota_made rows_made tables_turned tables_copied w_turned
        w_copied w_split base_turned fits_known pool_masked self_dve
        xa_turned xa_ready p_product p_ready
        iota_ready deg_away deg_distance deg_block deg_hot deg_counted deg_made deg_rooted
        dinv_made dinv_stored dinv_loaded dinv_turned dinv_ready agg_cleared
        p_index ea_rounded ea_turned ea_ready hidden_product hidden_upper hidden_ready
        gate_product gate_added gate_ready core_done core_biased msg_ready hot_ready scattered agg_added
        slow_hot slow_scattered slow_added
        win_copied win_turned x_loaded node_summed node_stats node_normed gamma_scaled sum_ready sum_stats sum_shift
        moments_ready deviations_ready scales_ready
        x3_ready g_ready g_turned g_back begun gathers_begun slow_begun dinv_squared
        hop_scaled hop_turned hop_ready
        logits_done logit_rows logit_top l_chain expd lse_ready y_added
        y_summed y_stats y_moments y_deviation y_scale y_shift y_ready""".split()
        S = {n: sem(n) for n in names}
        for h in range(4):
            S[f"y_stored{h}"] = sem(f"y_stored{h}")
        for k in range(2):
            for n in "index hot_ready scattered agg_added slow_hot slow_scattered slow_added".split():
                S[f"h{k}_{n}"] = sem(f"h{k}_{n}")
            for n in ("p_gathered", "ea_loaded", "p_stored", "g_stored", "hop_stored", "xa_loaded"):
                S[f"{n}{k}"] = sem(f"{n}{k}")
            for s in range(HOP_SLOTS):
                S[f"h{k}_gathered{s}"] = sem(f"h{k}_gathered{s}")

        def count_turns(i, half):
            first = COUNTS * i + half * (COUNTS // 2)
            return [d for d in (first + k for k in range(COUNTS // 2)) if not isinstance(d, int) or d < R]

        def tile_columns(table, d):
            return table[:, STEP * d:STEP * (d + 1)] if isinstance(d, int) else table[:, ds(STEP * d, STEP)]

        setup_dmas = [0]
        block = ctx.enter_context(nc.Block())

        def over_groups(engine, step, first, last):
            for g in range(first, 2):
                step(g // 2, g % 2)
            with engine.Fori(1, R - 2) as i:
                for s in range(2):
                    step(i, s)
            for g in range(NG - 4, last):
                step(g // 2, g % 2)

        def at_group(stage, i, s, lag):
            turn, slot = i + (s + lag) // 2, (s + lag) % 2
            if not isinstance(turn, int) or 0 <= 2 * turn + slot < NG:
                stage(turn, slot, 2 * turn + slot)

        def at_tiles(stage, i, s, lag):
            for j in range(TILES):
                stage(*ahead(i, s * TILES, lag * TILES + j))

        def ea_pieces(s, odd, upper):
            first = DE * ((odd + (not upper)) % 2)
            return ea_turned_sb[first:first + DE, s, :].rearrange("p (q b e) -> p q b e", b=2, e=P)[:, :, odd, :]

        def ea_bank(odd):
            return banks[DE * odd:DE * (odd + 1), 7, 0:2 * P].rearrange("p (q e) -> p q e", q=2)

        def over_nodes(engine, step, first, last):
            end = NN - 2 - (NN - 2) % 4
            for t in range(first, 8):
                step(t - t % 4, t % 4)
            with engine.Fori(8, end - 3, 4) as t:
                for u in range(4):
                    step(t, u)
            for t in range(end, last):
                step(t - t % 4, t % 4)

        def at_tile(stage, t, u, lag, end=NN, slots=2):
            if not isinstance(t, int) or 0 <= t + u + lag < end:
                stage(t + (u + lag), (u + lag) % slots)

        def x3_rows(t):
            return x3[:, t, :] if isinstance(t, int) else x3[:, ds(t, 1), :].rearrange("p a n -> p (a n)")

        def column(table, t):
            return table[:, t:t + 1] if isinstance(t, int) else table[:, ds(t, 1)]

        def node_rows(table, t):
            return table[ds(NODES * t, NODES), :] if not isinstance(t, int) else table[NODES * t:NODES * (t + 1), :]

        def node_cols(table, t):
            return table[:, :, ds(NODES * t, NODES)] if not isinstance(t, int) else table[:, :, NODES * t:NODES * (t + 1)]

        @block.sync
        def _(sp):
            def load(to, of):
                sp.dma_start(to, of).then_inc(S["setup_loaded"], 16)
                setup_dmas[0] += 1

            def load_rows(to, of):
                sp.dma_start(to, of).then_inc(S["rows_loaded"], 16)

            full = (R - 1) * 2 * GROUP
            for rows, index in ((dst_rows, dst), (src_rows, src)):
                load_rows(rows[0:R - 1, :, :], index[0:full].rearrange("(r s e) -> r s e", s=2, e=GROUP))
                load_rows(rows[R - 1:R, 0, :], index[full:full + GROUP].rearrange("(r e) -> r e", r=1))
                load_rows(rows[R - 1:R, 1, :], index[E - GROUP:E].rearrange("(r e) -> r e", r=1))
            for n, w in enumerate((W1, Wg)):
                cols = slice(n * H, (n + 1) * H)
                load(w_x[:, :, cols], w[0:H, :].rearrange("(k p) n -> p k n", p=P))
                load(w_e[0:DE, cols], w[H:H + DE, :])
                load(w_e[DE:P, cols], w[H:H + DE, :])
            load(bias_in[:, 0:H], b1.partition_broadcast(P))
            load(bias_in[:, H:H2], bg.partition_broadcast(P))
            load(w_2, W2.rearrange("(k p) n -> p k n", p=P))
            load(w_l[:, :, :], Wl.rearrange("(k p) n -> p k n", p=P))
            for to, of in ((bias_core, b2), (gamma_all, gamma), (beta_all, beta), (bias_l, bl)):
                load(to[:, :], of.partition_broadcast(P))

            def load_xa(i, h):
                t = 2 * i + h
                wait_count(sp, S["xa_turned"], t - 1)
                sp.dma_start(x_t[:, h, :], node_rows(x, t)).then_inc(S[f"xa_loaded{h}"], 16)

            def load_x3(i):
                rows = (x[2 * NODES * i:2 * NODES * (i + 1), :] if isinstance(i, int)
                        else x[ds(2 * NODES * i, 2 * NODES), :])
                to = x3[:, 2 * i:2 * (i + 1), :] if isinstance(i, int) else x3[:, ds(2 * i, 2), :]
                sp.dma_start(to, rows.rearrange("(t p) n -> p t n", p=NODES)).then_inc(S["x_loaded"], 16)

            for h in range(2):
                load_xa(0, h)
            sp.wait_ge(S["tables_turned"], 4)
            load_x3(0)
            with sp.Fori(1, NN // 2) as i:
                for h in range(2):
                    load_xa(i, h)
                load_x3(i)

            def load_ea(i, s):
                g = 2 * i + s
                wait_count(sp, S["ea_turned"], g - 1)
                if isinstance(g, int):
                    e0 = min(GROUP * g, E - GROUP)
                    rows = edge_attr[e0:e0 + GROUP, :]
                else:
                    rows = edge_attr[ds(GROUP * g, GROUP), :]
                sp.dma_start(ea[:, s, :, :], rows.rearrange("(p j) d -> p j d", j=TILES)).then_inc(
                    S[f"ea_loaded{s}"], 16)

            for s in range(2):
                load_ea(0, s)
            with sp.Fori(1, R // 2) as i:
                for s in range(2):
                    load_ea(i, s)

            sp.wait_ge(S["dinv_made"], 1)
            sp.dma_start(dinv_flat.rearrange("(b n) -> b n", n=P), dinv_rows[0:NB, :]).then_inc(S["dinv_stored"], 16)
            sp.wait_ge(S["dinv_stored"], 16)
            sp.dma_start(dinv_rows[0:NN, 0:NODES], dinv_flat[0:N].rearrange("(t p) -> t p", p=NODES)).then_inc(
                S["dinv_loaded"], 16)
            sp.dma_start(dinv_all[:, :], dinv_flat[0:N].partition_broadcast(P)).then_inc(S["dinv_loaded"], 16)

            with sp.Fori(R // 2, R - 1) as i:
                for s in range(2):
                    load_ea(i, s)
            for s in range(2):
                load_ea(R - 1, s)

            def store_g(i, h):
                t = 2 * i + h
                sp.wait_ge(S["g_ready"], t + 1)
                sp.dma_start(node_rows(hop_table[0], t), g_t[:, h, :]).then_inc(S[f"g_stored{h}"], 16)

            with sp.Fori(0, NN // 2) as i:
                for h in range(2):
                    store_g(i, h)

            with sp.Fori(0, NN // (2 * PART)) as i:
                for h in range(2):
                    sp.wait_ge(S["hop_ready"], PART * (2 * i + (h + 1)))
                    sp.dma_start(hop_table[1][ds(NODES * PART * (2 * i + h), NODES * PART), :].rearrange(
                        "(t p) n -> p t n", p=NODES), hop_out[:, h * PART:(h + 1) * PART, :]).then_inc(
                        S[f"hop_stored{h}"], 16)

            def store_y(t, h):
                sp.wait_ge(S["y_ready"], t + 1)
                sp.dma_start(node_rows(out, t), y_t[:, h, :]).then_inc(S[f"y_stored{h}"], 16)

            over_nodes(sp, lambda t, u: at_tile(store_y, t, u, 0, slots=4), 0, NN)
            for h in range(4):
                sp.wait_ge(S[f"y_stored{h}"], 16 * -(-(NN - h) // 4))

        @block.gpsimd
        def _(pool):
            nc.gpsimd.memset(ident[:, :], 0.0).then_inc(S["iota_made"], 1)
            nc.gpsimd.iota(iota_i[:, :], pattern=[[1, P]], base=0, channel_multiplier=0).then_inc(S["iota_made"], 1)
            nc.gpsimd.iota(block_i[:, :], pattern=[[-WINDOW, NB]], base=0, channel_multiplier=0).then_inc(
                S["iota_made"], 1)
            pool.wait_ge(S["iota_made"], 3)
            nc.gpsimd.affine_select(out=ident[:, :], in_=ident[:, :], compare_op=ALU.not_equal, fill=1.0, base=0,
                                    pattern=[[-1, P]], channel_multiplier=1).then_inc(S["consts_ready"], 1)
            nc.gpsimd.memset(moments[:, :, :, :], 1.0)
            nc.gpsimd.memset(eps[:, :], EPS).then_inc(S["consts_ready"], 1)
            nc.gpsimd.memset(agg[:, :, :], 0.0).then_inc(S["agg_cleared"], 1)

            pool.wait_ge(S["rows_made"], 1)
            if OVERLAP:
                for table in (1, 2):
                    rows = index_rows[0:R, table, 1, :]
                    nc.gpsimd.affine_select(
                        out=rows, in_=rows, compare_op=ALU.is_ge, fill=-1.0, base=(R - 1) * 2 * GROUP - OVERLAP,
                        pattern=[[1, GROUP]], channel_multiplier=-2 * GROUP).then_inc(S["pool_masked"], 1)

            def block_distances(i):
                for half in range(2):
                    for k, d in enumerate(count_turns(i, half)):
                        wait_count(pool, S["deg_counted"], d - COUNTS + 1)
                        nc.gpsimd.tensor_tensor(
                            hot_hi[:, half * (COUNTS // 2) + k, :, :],
                            iota_b[:, 0:NB].unsqueeze(1).to_broadcast([P, STEP, NB]),
                            tile_columns(hi_t, d).unsqueeze(2).to_broadcast([P, STEP, NB]),
                            ALU.subtract).then_inc(S["deg_away"], 1)

            pool.wait_ge(S["iota_ready"], 1)
            pool.wait_ge(S["tables_copied"], 4)
            over_setup(pool, block_distances, NN // 2)

            def gather(table, rows, slots, stored, index, done, free, each, stores, i, s):
                g = slots * i + s
                wait_count(pool, S[free], each * (g - slots + 1))
                if isinstance(g, int) and g == 0:
                    for h in range(2):
                        pool.wait_ge(S[f"{stored}{h}"], 16 * stores)
                pool.wait_ge(S[index], g + 1)
                pool.sem_inc(S["gathers_begun"], 1)
                for j in range(TILES):
                    pool.indirect_dma_start(
                        out=rows[:, s, j, :], out_offset=None, in_=table[:, :],
                        in_offset=bass.IndirectOffsetOnAxis(ap=index_now[:, s, j:j + 1], axis=0),
                    ).then_inc(S[f"{done}{s}"], 16)

            def gather_all(table, rows, slots, stored, index, done, free, each, stores):
                for s in range(slots):
                    gather(table, rows, slots, stored, index, done, free, each, stores, 0, s)
                with pool.Fori(1, NG // slots) as i:
                    for s in range(slots):
                        gather(table, rows, slots, stored, index, done, free, each, stores, i, s)

            gather_all(p_table, gathered, 2, "p_stored", "p_index", "p_gathered", "gate_added", 2, NN // 2)

            def add_beta(t, h):
                pool.wait_ge(S["node_summed"], t + 1)
                nc.gpsimd.tensor_tensor(x3_rows(t), x3_rows(t), beta_all[0:NODES, :], ALU.add)

            def scale_gamma(t, h):
                pool.wait_ge(S["node_normed"], t + 1)
                nc.gpsimd.tensor_tensor(node[:, h, :], node[:, h, :], gamma_all[0:NODES, :], ALU.mult).then_inc(
                    S["gamma_scaled"], 1)

            def node_step(i, u):
                at_tile(scale_gamma, i, u, -1)
                at_tile(add_beta, i, u, 0)

            over_nodes(pool, node_step, 0, NN + 1)

            gather_all(hop_table[0], hop_rows, HOP_SLOTS, "g_stored", "h0_index", "h0_gathered", "h0_scattered", TILES,
                       NN // 2)

            gather_all(hop_table[1], hop_rows, HOP_SLOTS, "hop_stored", "h1_index", "h1_gathered", "h1_scattered", TILES,
                       NN // (2 * PART))

        @block.tensor
        def _(pe):
            pe.wait_ge(S["consts_ready"], 1)
            pe.wait_ge(S["setup_loaded"], 16 * setup_dmas[0])

            for o in range(KC):
                for k in range(KC):
                    at = (k * KC + o) * P
                    last = nc.tensor.transpose(banks[:, 5, at:at + P], w_l[:, o, k * P:(k + 1) * P], ident[:, :])
            last.then_inc(S["w_turned"], 1)

            pe.wait_ge(S["rows_made"], 1)
            if OVERLAP:
                pe.wait_ge(S["pool_masked"], 2)
            for table in range(4):
                wait_count(pe, S["tables_copied"], table)
                for s in range(2):
                    for j in range(TILES):
                        last = nc.tensor.transpose(banks[:, 6 + s, j * R:(j + 1) * R],
                                                   index_rows[0:R, table, s, j:GROUP:TILES], ident[0:R, 0:R])
                last.then_inc(S["tables_turned"], 1)
            nc.tensor.transpose(banks[0:2, 4, 0:R], base_f[0:R, :], ident[0:R, 0:R])
            nc.tensor.transpose(banks[0:1, 4, P:P + R], span_max[0:R, :], ident[0:R, 0:R]).then_inc(S["base_turned"], 1)

            def turn_x(i, h):
                t = 2 * i + h
                pe.wait_ge(S[f"xa_loaded{h}"], 16 * (i + 1))
                wait_count(pe, S["xa_ready"], t - 1)
                for k in range(KC):
                    last = nc.tensor.transpose(banks[:, h, k * NODES:(k + 1) * NODES],
                                               x_t[:, h, k * P:(k + 1) * P], ident[0:NODES, 0:NODES])
                last.then_inc(S["xa_turned"], 1)

            def product_x(i, h):
                t = 2 * i + h
                pe.wait_ge(S["xa_ready"], t + 1)
                wait_count(pe, S["p_ready"], t - 1)
                for k in range(KC):
                    last = nc.tensor.matmul(banks[0:NODES, 2 + h, :], x_turned_sb[:, h, k, :], w_x[:, k, :],
                                            start=k == 0, stop=k == KC - 1)
                last.then_inc(S["p_product"], 1)

            def count(i, half):
                for k, d in enumerate(count_turns(i, half)):
                    slot = half * (COUNTS // 2) + k
                    pe.wait_ge(S["deg_hot"], d + 1)
                    pe.wait_ge(S["deg_block"], d + 1)
                    for u in range(STEP):
                        last = nc.tensor.matmul(banks[0:NB, 4, 0:P], hot_hi[:, slot, u, :], hot_lo[slot][:, u, :],
                                                start=isinstance(d, int) and d == 0 and u == 0,
                                                stop=isinstance(d, int) and d == R - 1 and u == STEP - 1,
                                                skip_group_check=True)
                    last.then_inc(S["deg_counted"], 1)

            def node_turn(i):
                for h in range(2):
                    if not isinstance(i, int) or i >= 1:
                        product_x(i - 1, h)
                    turn_x(i, h)
                    count(i, h)

            pe.wait_ge(S["fits_known"], 1)
            over_setup(pe, node_turn, NN // 2)
            for h in range(2):
                product_x(NN // 2 - 1, h)

            pe.wait_ge(S["xa_ready"], NN)
            pe.wait_ge(S["p_ready"], NN)
            pe.wait_ge(S["dinv_made"], 1)
            pe.wait_ge(S["w_copied"], 1)
            pe.wait_ge(S["tables_copied"], 4)
            pe.wait_ge(S["w_split"], 2)

            def turn_ea(turn, s, g):
                pe.wait_ge(S[f"ea_loaded{s}"], 16 * (turn + 1))
                wait_count(pe, S["ea_ready"], 2 * g)
                for q in range(2):
                    last = nc.tensor.transpose(banks[:, 7, q * P:(q + 1) * P],
                                               ea[:, s, 2 * q:2 * q + 2, :].rearrange("p j d -> p (j d)"), ident[:, :])
                last.then_inc(S["ea_turned"], 1)

            def hidden_product(turn, s, g):
                pe.wait_ge(S["ea_ready"], 2 * (g + 1))
                pe.wait_ge(S[f"p_gathered{s}"], 16 * TILES * (turn + 1))
                for k in range(KC):
                    columns = slice(k * P, (k + 1) * P)
                    wait_count(pe, S["hidden_ready"], 2 * g + k - 1)
                    nc.tensor.matmul(banks[:, k, :], w_e_hi[:, columns], ea_turned_sb[:, s, :], start=True, stop=False)
                    nc.tensor.matmul(banks[:, k, :], w_e_lo[:, columns], ea_turned_sb[:, s, :], start=False, stop=False)
                    for j in range(TILES):
                        last = nc.tensor.matmul(banks[:, k, j * P:(j + 1) * P], gathered[:, s, j, columns], ident[:, :],
                                                start=False, stop=j == TILES - 1, is_transpose=True)
                    last.then_inc(S["hidden_product"], 1)

            def gate_product(turn, s, g):
                for half in range(2):
                    wait_count(pe, S["gate_added"], 2 * g + half - 1)
                    for j in range(2 * half, 2 * half + 2):
                        to, lhs = banks[:, 2 + half, j % 2 * H:(j % 2 + 1) * H], ea_turned_sb[:, s, j * P:(j + 1) * P]
                        nc.tensor.matmul(to, lhs, w_e_hi[:, H:H2], start=True, stop=False)
                        last = nc.tensor.matmul(to, lhs, w_e_lo[:, H:H2], start=False, stop=True)
                    last.then_inc(S["gate_product"], 1)

            def core_product(turn, s, g):
                pe.wait_ge(S["hidden_ready"], KC * (g + 1))
                for half in range(2):
                    wait_count(pe, S["core_biased"], 2 * g + half - 1)
                    for j in range(2 * half, 2 * half + 2):
                        products = [(a[:, k, j * P:(j + 1) * P], b[:, k, :]) for k in range(KC)
                                    for a, b in ((hidden_hi, w_2_hi), (hidden_hi, w_2_lo), (hidden_lo, w_2_hi))]
                        for n, (lhs, rhs) in enumerate(products):
                            last = nc.tensor.matmul(banks[:, 4 + half, j % 2 * H:(j % 2 + 1) * H], lhs, rhs,
                                                    start=n == 0, stop=n == len(products) - 1)
                    last.then_inc(S["core_done"], 1)

            def scatter(rows_of, ready, hop, turn, u, t, g):
                if isinstance(t, int) and not 0 <= t < NT:
                    return
                j = u % TILES
                ready(turn, u, t, g)
                if j == 0:
                    pe.wait_ge(S[hop + "hot_ready"], g + 1)
                    wait_count(pe, S[hop + "agg_added"], g)
                for k in range(KC):
                    last = nc.tensor.matmul(banks[:, 6, k * WINDOW:(k + 1) * WINDOW],
                                            rows_of(u)[:, k * P:(k + 1) * P], hot[:, u % STEP, :],
                                            start=j == 0 and k == 0, stop=j == TILES - 1, skip_group_check=True)
                last.then_inc(S[hop + "scattered"], 1)

            def scatter_anywhere(rows_of, ready, hop, turn, u, t, g):
                if isinstance(t, int) and not 0 <= t < NT:
                    return
                ready(turn, u, t, g)
                if u % TILES < TILES - 1:
                    return
                pe.sem_inc(S["slow_begun"], 1)
                with pe.Fori(0, NB) as w:
                    pe.wait_ge(S[hop + "slow_hot"], g * NB + w + 1)
                    pe.wait_ge(S[hop + "slow_added"], g * NB + w + 1)
                    for jj in range(TILES):
                        uu = u - TILES + 1 + jj
                        for k in range(KC):
                            last = nc.tensor.matmul(banks[:, 6, k * WINDOW:(k + 1) * WINDOW],
                                                    rows_of(uu)[:, k * P:(k + 1) * P], hot[:, uu % STEP, :],
                                                    start=jj == 0 and k == 0, stop=jj == TILES - 1,
                                                    skip_group_check=True)
                    last.then_inc(S[hop + "slow_scattered"], 1)

                pe.wait_ge(S[hop + "slow_added"], (g + 1) * NB + 1)
                for _ in range(TILES):
                    pe.sem_inc(S[hop + "scattered"], 1)

            def msg_of(u):
                return msg[:, u, :]

            def msg_is_ready(turn, u, t, g):
                if u % 2 == 0:
                    pe.wait_ge(S["msg_ready"], 2 * g + u % TILES // 2 + 1)

            def edge_steps(scatter_stage):
                def step(i, s):
                    at_group(core_product, i, s, 0)
                    at_group(hidden_product, i, s, 1)
                    at_group(gate_product, i, s, 1)
                    at_tiles(lambda *tile: scatter_stage(msg_of, msg_is_ready, "", *tile), i, s, 0)
                    at_group(turn_ea, i, s, 3)
                over_groups(pe, step, -3, NG)

            in_order = pe.value_load(fits[0:1, 0:1], min_val=0, max_val=1)
            with pe.If(in_order):
                edge_steps(scatter)
            with pe.Else():
                edge_steps(scatter_anywhere)

            def turn_win(t, h):
                pe.wait_ge(S["win_copied"], t + 1)
                wait_count(pe, S["node_summed"], t - 1)
                for k in range(KC):
                    last = nc.tensor.transpose(banks[0:NODES, h, k * P:(k + 1) * P], x_turned_sb[:, h, k, :],
                                               ident[:, :])
                last.then_inc(S["win_turned"], 1)

            def turn_g(t, h):
                pe.wait_ge(S["g_ready"], t + 1)
                wait_count(pe, S["g_back"], t - 1)
                for k in range(KC):
                    last = nc.tensor.transpose(banks[:, 2 + h, k * NODES:(k + 1) * NODES],
                                               g_t[:, h, k * P:(k + 1) * P], ident[0:NODES, 0:NODES])
                last.then_inc(S["g_turned"], 1)

            pe.wait_ge(S["agg_added"], NG)
            pe.wait_ge(S["dinv_loaded"], 32)
            nc.tensor.transpose(banks[0:NODES, 4, 0:NN], dinv_rows[0:NN, 0:NODES], ident[0:NN, 0:NN]).then_inc(
                S["dinv_turned"], 1)
            def node_step(i, u):
                at_tile(turn_win, i, u, 1)
                at_tile(turn_g, i, u, -3)

            over_nodes(pe, node_step, -1, NN + 3)

            def hop_steps(k, scatter_stage):
                def rows_of(u):
                    return hop_rows[:, u // TILES, u % TILES, :]

                def are_gathered(turn, u, t, g):
                    if u % TILES == 0:
                        pe.wait_ge(S[f"h{k}_gathered{u // TILES}"], 16 * TILES * (turn + 1))

                def step(i, u):
                    scatter_stage(rows_of, are_gathered, f"h{k}_", *ahead(i, u, 0, HOP_STEP))
                over_tiles(pe, step, 0, NT, HR, HOP_STEP)

            for k in range(2):
                with pe.If(in_order):
                    hop_steps(k, scatter)
                with pe.Else():
                    hop_steps(k, scatter_anywhere)
                if k == 0:
                    def turn_hop(t, h):
                        pe.wait_ge(S["win_copied"], NN + t + 1)
                        wait_count(pe, S["hop_ready"], t - 1)
                        for c in range(KC):
                            last = nc.tensor.transpose(banks[0:NODES, h, c * P:(c + 1) * P], x_turned_sb[:, h, c, :],
                                                       ident[:, :])
                        last.then_inc(S["hop_turned"], 1)

                    for h in range(2):
                        turn_hop(h, h)
                    with pe.Fori(1, NN // 2) as i:
                        for h in range(2):
                            turn_hop(2 * i + h, h)

            def logits(t, h):
                pe.wait_ge(S["win_copied"], 2 * NN + t + 1)
                wait_count(pe, S["logit_rows"], t - 1)
                for k in range(KC):
                    last = nc.tensor.matmul(banks[0:NODES, h, 0:H], x_turned_sb[:, h, k, :], w_l_turned[:, k, :],
                                            start=k == 0, stop=k == KC - 1)
                last.then_inc(S["logits_done"], 1)

            for h in range(2):
                logits(h, h)
            with pe.Fori(1, NN // 2) as i:
                for h in range(2):
                    logits(2 * i + h, h)

        @block.scalar
        def _(act):
            def copy_x(i, h):
                t = 2 * i + h
                act.wait_ge(S["xa_turned"], t + 1)
                wait_count(act, S["p_product"], t - 1)
                nc.scalar.copy(x_turned_sb[:, h, :, :].rearrange("p k n -> p (k n)"),
                               banks[:, h, 0:KC * NODES]).then_inc(S["xa_ready"], 1)

            def store_p(i, h):
                t = 2 * i + h
                act.wait_ge(S["p_ready"], t + 1)
                act.dma_start(node_rows(p_table, t), p_t[:, h, :]).then_inc(S[f"p_stored{h}"], 16)

            def blocks_hot(i, half):
                counts = count_turns(i, half)
                if not counts:
                    return
                first = half * (COUNTS // 2)
                rows = hot_hi[:, first:first + len(counts), :, :].rearrange("p d u n -> p (d u n)")
                act.wait_ge(S["deg_away"], counts[-1] + 1)
                nc.scalar.activation(rows, rows, ACT.Abs).then_inc(S["deg_distance"], len(counts))
                act.wait_ge(S["deg_distance"], counts[-1] + 1)
                nc.scalar.activation(rows, rows, ACT.Relu, scale=-1.0, bias=iota[:, 1:2]).then_inc(
                    S["deg_block"], len(counts))

            def node_turn(i):
                for h in range(2):
                    copy_x(i, h)
                    blocks_hot(i + (h + 1) // 2, (h + 1) % 2)
                    if not isinstance(i, int) or i >= 1:
                        store_p(i - 1, h)

            blocks_hot(0, 0)
            over_setup(act, node_turn, NN // 2)
            for h in range(2):
                store_p(NN // 2 - 1, h)

            act.wait_ge(S["deg_made"], 1)
            nc.scalar.activation(dinv_rows[0:NB, :], dinv_rows[0:NB, :], ACT.Sqrt).then_inc(S["deg_rooted"], 1)

            def copy_index(index, gathered, slots, turn, s):
                if isinstance(turn, int) and turn >= NG // slots:
                    return
                wait_count(act, S[f"{gathered}{s}"], 16 * TILES * turn)
                c = TILES * (slots * turn + s)
                columns = src_t[:, c:c + TILES] if isinstance(c, int) else src_t[:, ds(c, TILES)]
                nc.scalar.copy(index_now[:, s, :], columns).then_inc(S[index], 1)

            def upper_ea(turn, s, g):
                act.wait_ge(S["ea_turned"], g + 1)
                wait_count(act, S["gate_product"], 2 * (g - 1))
                for odd in range(2):
                    nc.scalar.copy(ea_pieces(s, odd, True), ea_bank(odd)).then_inc(S["ea_rounded"], 1)

            def upper_hidden(turn, s, g):
                wait_count(act, S["core_done"], 2 * g)
                for k in range(KC):
                    act.wait_ge(S["hidden_product"], 2 * g + k + 1)
                    nc.scalar.activation(hidden_hi[:, k, :], banks[:, k, :], ACT.Relu).then_inc(S["hidden_upper"], 1)

            def open_gate(turn, s, g):
                for half in range(2):
                    act.wait_ge(S["gate_added"], 2 * g + half + 1)
                    rows = gate[:, 2 * half:2 * half + 2, :]
                    nc.scalar.activation(rows, rows, ACT.Sigmoid).then_inc(S["gate_ready"], 1)

            def step(i, s):
                at_group(upper_ea, i, s, 2)
                if not (isinstance(i, int) and i < 0):
                    copy_index("p_index", "p_gathered", 2, i + 1, s)
                at_group(upper_hidden, i, s, 1)
                at_group(open_gate, i, s, 1)

            act.wait_ge(S["tables_copied"], 4)
            for s in range(2):
                copy_index("p_index", "p_gathered", 2, 0, s)
            over_groups(act, step, -3, NG)

            def copy_win(turned):
                def stage(t, h):
                    wait_count(act, S[turned], t - 1)
                    if turned == "hop_turned":
                        act.wait_ge(S["hop_scaled"], t + 1)
                    nc.scalar.copy(x_turned_sb[:, h, :, :], node_cols(agg, t)).then_inc(S["win_copied"], 1)
                return stage

            def deviations(t, h):
                act.wait_ge(S["moments_ready"], t + 1)
                nc.scalar.activation(scale[:, :, h], moments[:, :, h, 1], ACT.Sqrt, bias=eps[:, :]).then_inc(
                    S["deviations_ready"], 1)

            def last_deviation(t, h):
                act.wait_ge(S["y_moments"], t + 1)
                nc.scalar.activation(last_scale[:, h:h + 1], last_moments_t[:, h, 1:2], ACT.Sqrt,
                                     bias=eps[:, :]).then_inc(S["y_deviation"], 1)

            def normalise(n, rows, result, h):
                return nc.scalar.activation(result, rows, ACT.Identity, scale=scale[:, n, h:h + 1],
                                            bias=shift[:, n, h:h + 1])

            def second_norm(t, h):
                act.wait_ge(S["sum_shift"], t + 1)
                normalise(1, sum_t[:, h, :], x3_rows(t), h).then_inc(S["x3_ready"], 1)

            def scale_g(t, h):
                act.wait_ge(S["x3_ready"], t + 1)
                wait_count(act, S[f"g_stored{h}"], 8 * (t - h))
                nc.scalar.activation(g_t[:, h, :], x3_rows(t), ACT.Copy, scale=column(dinv_col, t)).then_inc(
                    S["g_ready"], 1)

            def back_g(t, h):
                act.wait_ge(S["g_turned"], t + 1)
                nc.scalar.copy(node_cols(agg, t), banks[:, 2 + h, 0:KC * NODES].rearrange("p (k n) -> p k n", k=KC)
                               ).then_inc(S["g_back"], 1)

            def node_step(i, u):
                at_tile(copy_win("win_turned"), i, u, 1)
                at_tile(second_norm, i, u, -3)
                at_tile(back_g, i, u, -4)
                at_tile(scale_g, i, u, -3)
                at_tile(deviations, i, u, 0, NN + 2)

            act.wait_ge(S["agg_added"], NG)
            act.wait_ge(S["dinv_turned"], 1)
            nc.scalar.copy(dinv_col[:, :], banks[0:NODES, 4, 0:NN]).then_inc(S["dinv_ready"], 1)
            act.wait_ge(S["dinv_ready"], 1)
            act.wait_ge(S["consts_ready"], 2)
            over_nodes(act, node_step, -1, NN + 4)

            for s in range(HOP_SLOTS):
                copy_index("h0_index", "h0_gathered", HOP_SLOTS, 0, s)
            with act.Fori(1, HR) as i:
                for s in range(HOP_SLOTS):
                    copy_index("h0_index", "h0_gathered", HOP_SLOTS, i, s)

            def hop_step(i, u):
                t = 2 * PART * i
                at_tile(copy_win("hop_turned"), t, u, 1)
                if isinstance(t, int) and t + u < 0:
                    return
                act.wait_ge(S["hop_turned"], t + (u + 1))
                if u % PART == 0:
                    wait_count(act, S[f"hop_stored{u // PART}"], 16 * i)
                nc.scalar.copy(hop_out[:, u, :], banks[0:NODES, u % 2, 0:H]).then_inc(S["hop_ready"], 1)

            turns = NN // (2 * PART)
            for u in range(-1, 2 * PART):
                hop_step(0, u)
            with act.Fori(1, turns - 1) as i:
                for u in range(2 * PART):
                    hop_step(i, u)
            for u in range(2 * PART):
                hop_step(turns - 1, u)

            for s in range(HOP_SLOTS):
                copy_index("h1_index", "h1_gathered", HOP_SLOTS, 0, s)
            with act.Fori(1, HR) as i:
                for s in range(HOP_SLOTS):
                    copy_index("h1_index", "h1_gathered", HOP_SLOTS, i, s)

            def exponentials(t, h):
                act.wait_ge(S["l_chain"], t + 1)
                wait_count(act, S["expd"], t - 1)
                nc.scalar.activation(expo[:, h % 2, :], logit_rows_t[:, h, :], ACT.Exp, bias=top[:, h, 1:2],
                                     accum_out=column(sums, t)).then_inc(S["expd"], 1)

            def logit_step(i, u):
                at_tile(exponentials, i, u, -2, slots=4)
                at_tile(copy_win("logits_done"), i, u, 1)

            act.wait_ge(S["h1_agg_added"], NG)
            over_nodes(act, logit_step, -1, NN + 2)
            act.wait_ge(S["expd"], NN)
            nc.scalar.activation(lse[:, :], sums[:, :], ACT.Ln).then_inc(S["lse_ready"], 1)

            def last_norm(t, h):
                act.wait_ge(S["y_shift"], t + 1)
                wait_count(act, S[f"y_stored{h}"], 4 * (t - h))
                nc.scalar.activation(y_t[:, h, :], logit_rows_t[:, h, :], ACT.Identity, scale=last_scale[:, h:h + 1],
                                     bias=last_shift[:, h:h + 1]).then_inc(S["y_ready"], 1)

            def last_step(i, u):
                at_tile(last_norm, i, u, -3, slots=4)
                at_tile(last_deviation, i, u, -1, slots=4)

            over_nodes(act, last_step, 0, NN + 3)

        @block.vector
        def _(dve):
            done = [0]

            def then(instruction):
                done[0] += 1
                instruction.then_inc(S["self_dve"], 1)
                dve.wait_ge(S["self_dve"], done[0])

            dve.wait_ge(S["rows_loaded"], 6 * 16)
            nc.vector.tensor_copy(dst_f[0:R, :, :], dst_rows[0:R, :, :])
            nc.vector.tensor_copy(index_rows[0:R, 0, :, :], src_rows[0:R, :, :])
            nc.vector.tensor_single_scalar(hi_i[0:R, :, :], dst_rows[0:R, :, :], WINDOW.bit_length() - 1,
                                           ALU.arith_shift_right)
            then(nc.vector.tensor_single_scalar(lo_i[0:R, :, :], dst_rows[0:R, :, :], WINDOW - 1, ALU.bitwise_and))
            nc.vector.tensor_copy(index_rows[0:R, 2, :, :], hi_i[0:R, :, :])
            nc.vector.tensor_copy(index_rows[0:R, 3, :, :], lo_i[0:R, :, :])
            nc.vector.tensor_reduce(base_f[0:R, :], dst_f[0:R, :, :], AX.X, ALU.min)
            then(nc.vector.tensor_reduce(top_f[0:R, :], dst_f[0:R, :, :], AX.X, ALU.max))
            then(nc.vector.tensor_tensor(span_f[0:R, :], top_f[0:R, :], base_f[0:R, :], ALU.subtract))
            then(nc.vector.tensor_reduce(span_max[0:R, :], span_f[0:R, :], AX.X, ALU.max))
            nc.vector.tensor_tensor(index_rows[0:R, 1, :, :], dst_f[0:R, :, :],
                                    base_f[0:R, :].unsqueeze(2).to_broadcast([R, 2, GROUP]),
                                    ALU.subtract).then_inc(S["rows_made"], 1)
            dve.wait_ge(S["iota_made"], 3)
            nc.vector.tensor_copy(block_starts[:, :], block_i[:, :])
            nc.vector.tensor_copy(iota[:, :], iota_i[:, :])
            nc.vector.tensor_copy(iota_b[:, :], iota_i[:, :]).then_inc(S["iota_ready"], 1)
            dve.wait_ge(S["setup_loaded"], 16 * setup_dmas[0])
            then(nc.vector.tensor_copy(w_e_hi[:, :], w_e[:, :]))
            nc.vector.tensor_tensor(w_e_lo[:, :], w_e[:, :], w_e_hi[:, :].bitcast(F32), ALU.subtract).then_inc(
                S["w_split"], 1)
            then(nc.vector.tensor_copy(w_2_hi[:, :, :], w_2))
            nc.vector.tensor_tensor(w_2_lo[:, :, :], w_2, w_2_hi[:, :, :].bitcast(F32), ALU.subtract).then_inc(
                S["w_split"], 1)
            dve.wait_ge(S["w_turned"], 1)
            nc.vector.tensor_copy(w_l_turned[:, :, :].rearrange("p k n -> p (k n)"), banks[:, 5, :]).then_inc(
                S["w_copied"], 1)
            for n, table in enumerate((src_t, local_t, hi_t, lo_t)):
                dve.wait_ge(S["tables_turned"], n + 1)
                by_tile = table[:, :].rearrange("p (i s j) -> p i s j", s=2, j=TILES)
                for s in range(2):
                    last = nc.vector.tensor_copy(by_tile[:, :, s, :],
                                                 banks[:, 6 + s, 0:TILES * R].rearrange("p (j i) -> p i j", j=TILES))
                last.then_inc(S["tables_copied"], 1)
            dve.wait_ge(S["tables_copied"], 4)
            dve.wait_ge(S["base_turned"], 1)
            nc.vector.tensor_copy(bases[:, :], banks[0:2, 4, 0:R])
            then(nc.vector.tensor_reduce(widest[:, :], banks[0:1, 4, P:P + R], AX.X, ALU.max))
            nc.vector.tensor_single_scalar(fits[:, :], widest[:, :], float(WINDOW), ALU.is_lt).then_inc(
                S["fits_known"], 1)

            def bias_p(i, h):
                t = 2 * i + h
                dve.wait_ge(S["p_product"], t + 1)
                wait_count(dve, S[f"p_stored{h}"], 8 * (t - h))
                nc.vector.tensor_tensor(p_t[:, h, :], banks[0:NODES, 2 + h, :], bias_in[0:NODES, :],
                                        ALU.add).then_inc(S["p_ready"], 1)

            def node_turn(i):
                for half in range(2):
                    for k, d in enumerate(count_turns(i, half)):
                        wait_count(dve, S["deg_counted"], d - COUNTS + 1)
                        slot = half * (COUNTS // 2) + k
                        nc.vector.tensor_tensor(
                            hot_lo[slot], iota_b[:, :].unsqueeze(1).to_broadcast([P, STEP, P]),
                            tile_columns(lo_t, d).unsqueeze(2).to_broadcast([P, STEP, P]),
                            ALU.is_equal).then_inc(S["deg_hot"], 1)
                    if not isinstance(i, int) or i >= 1:
                        bias_p(i - 1, half)

            over_setup(dve, node_turn, NN // 2)
            for h in range(2):
                bias_p(NN // 2 - 1, h)
            dve.wait_ge(S["deg_counted"], R)
            nc.vector.tensor_single_scalar(dinv_rows[0:NB, :], banks[0:NB, 4, 0:P], 1.0, ALU.add).then_inc(
                S["deg_made"], 1)

            dst_t = hi_t
            then(nc.vector.scalar_tensor_tensor(out=dst_t[:, :], in0=hi_t[:, :], scalar=float(WINDOW), in1=lo_t[:, :],
                                                op0=ALU.mult, op1=ALU.add))

            dve.wait_ge(S["deg_rooted"], 1)
            nc.vector.reciprocal(dinv_rows[0:NB, :], dinv_rows[0:NB, :]).then_inc(S["dinv_made"], 1)

            def lower_ea(turn, s, g):
                for odd in range(2):
                    dve.wait_ge(S["ea_rounded"], 2 * g + odd + 1)
                    nc.vector.tensor_tensor(ea_pieces(s, odd, False), ea_bank(odd),
                                            ea_pieces(s, odd, True).bitcast(F32), ALU.subtract).then_inc(
                        S["ea_ready"], 1)

            def lower_hidden(k):
                def stage(turn, s, g):
                    dve.wait_ge(S["hidden_upper"], 2 * g + k + 1)
                    nc.vector.scalar_tensor_tensor(out=hidden_lo[:, k, :], in0=banks[:, k, :], scalar=0.0,
                                                   in1=hidden_hi[:, k, :].bitcast(F32), op0=ALU.max,
                                                   op1=ALU.subtract).then_inc(S["hidden_ready"], 1)
                return stage

            def add_gate(turn, s, g):
                wait_count(dve, S["msg_ready"], 2 * g)
                for half in range(2):
                    dve.wait_ge(S["gate_product"], 2 * g + half + 1)
                    tiles = slice(2 * half, 2 * half + 2)
                    nc.vector.tensor_tensor(gate[:, tiles, :], banks[:, 2 + half, :].rearrange("p (j n) -> p j n", j=2),
                                            gathered[:, s, tiles, H:H2], ALU.add).then_inc(S["gate_added"], 1)

            def message(turn, s, g):
                wait_count(dve, S["scattered"], TILES * (g - 1))
                for half in range(2):
                    dve.wait_ge(S["core_done"], 2 * g + half + 1)
                    wait_count(dve, S["msg_ready"], 2 * g + half)
                    nc.vector.tensor_tensor(core[:, :, :], banks[:, 4 + half, :].rearrange("p (j n) -> p j n", j=2),
                                            bias_core[:, :].unsqueeze(1).to_broadcast([P, 2, H]), ALU.add).then_inc(
                        S["core_biased"], 1)
                    dve.wait_ge(S["core_biased"], 2 * g + half + 1)
                    dve.wait_ge(S["gate_ready"], 2 * g + half + 1)
                    u = TILES * s + 2 * half
                    nc.vector.tensor_tensor(msg[:, u:u + 2, :], core[:, :, :], gate[:, 2 * half:2 * half + 2, :],
                                            ALU.mult).then_inc(S["msg_ready"], 1)

            def one_hot(hop, turn, u, t, g):
                if isinstance(t, int) and not 0 <= t < NT or u % TILES:
                    return
                wait_count(dve, S[hop + "scattered"], t - TILES)
                columns = local_t[:, t:t + TILES] if isinstance(t, int) else local_t[:, ds(t, TILES)]
                nc.vector.tensor_tensor(hot[:, u % STEP:u % STEP + TILES, :],
                                        iota[:, 0:WINDOW].unsqueeze(1).to_broadcast([P, TILES, WINDOW]),
                                        columns.unsqueeze(2).to_broadcast([P, TILES, WINDOW]),
                                        ALU.is_equal).then_inc(S[hop + "hot_ready"], 1)

            def add_window(hop, turn, u, t, g):
                if isinstance(t, int) and not 0 <= t < NT:
                    return
                if u % TILES < TILES - 1:
                    return
                s, pair_of = u // TILES % 2, (STEP if hop == "" else HOP_STEP) // STEP * turn + u // STEP
                at = bases[s:s + 1, pair_of:pair_of + 1] if isinstance(turn, int) else bases[s:s + 1, ds(pair_of, 1)]
                base = dve.value_load(at, min_val=0, max_val=N - 1)
                dve.wait_ge(S[hop + "scattered"], TILES * (g + 1))
                wait_count(dve, S[hop + "agg_added"], g)
                where = agg[:, :, ds(base, WINDOW)]
                nc.vector.tensor_tensor(where, where, banks[:, 6, 0:KC * WINDOW].rearrange("p (k n) -> p k n", k=KC),
                                        ALU.add).then_inc(S[hop + "agg_added"], 1)

            def no_one_hot(hop, turn, u, t, g):
                pass

            def add_anywhere(hop, turn, u, t, g):
                if isinstance(t, int) and not 0 <= t < NT:
                    return
                j = u % TILES
                if j < TILES - 1:
                    return
                with dve.Fori(0, NB) as w:
                    dve.wait_ge(S[hop + "slow_added"], g * NB + w + 1)
                    for jj in range(TILES):
                        last = nc.vector.tensor_scalar(hot[:, (u - j + jj) % STEP, :], iota[:, 0:WINDOW],
                                                       column(dst_t, t - j + jj), block_starts[:, ds(w, 1)],
                                                       ALU.subtract, ALU.is_equal)
                    last.then_inc(S[hop + "slow_hot"], 1)
                    dve.wait_ge(S[hop + "slow_scattered"], g * NB + w + 1)
                    where = agg[:, :, ds(WINDOW * w, WINDOW)]
                    nc.vector.tensor_tensor(where, where,
                                            banks[:, 6, 0:KC * WINDOW].rearrange("p (k n) -> p k n", k=KC),
                                            ALU.add).then_inc(S[hop + "slow_added"], 1)
                dve.wait_ge(S[hop + "slow_added"], (g + 1) * NB + 1)
                dve.sem_inc(S[hop + "agg_added"], 1)

            def edge_steps(hot_stage, add_stage):
                def step(i, s):
                    at_tiles(lambda *tile: add_stage("", *tile), i, s, -1)
                    at_tiles(lambda *tile: hot_stage("", *tile), i, s, 0)
                    at_group(lower_ea, i, s, 2)
                    at_group(message, i, s, 0)
                    at_group(lower_hidden(0), i, s, 1)
                    at_group(add_gate, i, s, 1)
                    at_group(lower_hidden(1), i, s, 1)
                over_groups(dve, step, -3, NG + 1)

            def hop_steps(hop, hot_stage, add_stage):
                def step(i, u):
                    if u % TILES == 0:
                        for j in range(TILES):
                            hot_stage(hop, *ahead(i, u, TILES + j, HOP_STEP))
                    add_stage(hop, *ahead(i, u, 0, HOP_STEP))
                over_tiles(dve, step, -TILES, NT, HR, HOP_STEP)

            in_order = dve.value_load(fits[0:1, 0:1], min_val=0, max_val=1)
            dve.wait_ge(S["agg_cleared"], 1)
            with dve.If(in_order):
                edge_steps(one_hot, add_window)
            with dve.Else():
                dve.sem_inc(S["slow_added"], 1)
                edge_steps(no_one_hot, add_anywhere)

            def reciprocals(t, h):
                dve.wait_ge(S["deviations_ready"], t + 1)
                nc.vector.reciprocal(scale[:, :, h], scale[:, :, h]).then_inc(S["scales_ready"], 1)

            def less_mean(n, scaled, shifted, later):
                def stage(t, h):
                    dve.wait_ge(S[scaled], t + (later + 1))
                    nc.vector.scalar_tensor_tensor(out=shift[:, n, h:h + 1], in0=moments[:, n, h, 0:1], scalar=-1.0,
                                                   in1=scale[:, n, h:h + 1], op0=ALU.mult, op1=ALU.mult).then_inc(
                        S[shifted], 1)
                return stage

            def first_norm(t, h):
                dve.wait_ge(S["scales_ready"], t + 1)
                nc.vector.tensor_scalar(node[:, h, :], node[:, h, :], moments[:, 0, h, 0:1], scale[:, 0, h:h + 1],
                                        ALU.subtract, ALU.mult).then_inc(S["node_normed"], 1)

            def first_statistics(t, h):
                dve.wait_ge(S["node_summed"], t + 1)
                nc.vector.bn_stats(stats[:, 0, h, :], node[:, h, :]).then_inc(S["node_stats"], 1)

            def second_statistics(t, h):
                dve.wait_ge(S["sum_ready"], t + 1)
                nc.vector.bn_stats(stats[:, 1, h, :], sum_t[:, h, :]).then_inc(S["sum_stats"], 1)

            def moments_of_both(t, h):
                first, second = not isinstance(t, int) or t < NN, not isinstance(t, int) or t >= 2
                if second:
                    if not first:
                        dve.wait_ge(S["sum_stats"], t - 1)
                        dve.sem_inc(S["begun"], 1)
                    last = nc.vector.bn_aggr(moments[:, 1, h, :], stats[:, 1, h, :])
                if first:
                    dve.wait_ge(S["node_stats"], t + 1)
                    dve.sem_inc(S["begun"], 1)
                    last = nc.vector.bn_aggr(moments[:, 0, h, :], stats[:, 0, h, :])
                last.then_inc(S["moments_ready"], 1)

            def first_sum(t, h):
                dve.wait_ge(S["win_turned"], t + 1)
                nc.vector.tensor_tensor(node[:, h, :], banks[0:NODES, h, 0:H], x3_rows(t), ALU.add).then_inc(
                    S["node_summed"], 1)

            def second_sum(t, h):
                wait_count(dve, S["x3_ready"], t - 1)
                dve.wait_ge(S["gamma_scaled"], t + 1)
                nc.vector.tensor_tensor(sum_t[:, h, :], node[:, h, :], x3_rows(t), ALU.add).then_inc(S["sum_ready"], 1)

            def node_step(i, u):
                at_tile(second_sum, i, u, -2)
                at_tile(reciprocals, i, u, -1, NN + 2)
                at_tile(first_norm, i, u, -1)
                at_tile(less_mean(1, "scales_ready", "sum_shift", 2), i, u, -3)
                at_tile(second_statistics, i, u, -2)
                at_tile(first_sum, i, u, 0)
                at_tile(first_statistics, i, u, 0)
                at_tile(moments_of_both, i, u, 0, NN + 2)

            dve.wait_ge(S["x_loaded"], 16 * (NN // 2))
            over_nodes(dve, node_step, 0, NN + 3)

            dve.wait_ge(S["dinv_loaded"], 32)
            nc.vector.tensor_tensor(dinv_all[:, :], dinv_all[:, :], dinv_all[:, :], ALU.mult).then_inc(
                S["dinv_squared"], 1)
            dve.wait_ge(S["g_back"], NN)
            for k in range(2):
                hop = f"h{k}_"
                with dve.If(in_order):
                    hop_steps(hop, one_hot, add_window)
                with dve.Else():
                    dve.sem_inc(S[hop + "slow_added"], 1)
                    hop_steps(hop, no_one_hot, add_anywhere)
                if k == 0:
                    def scale_hop(t, h):
                        where = node_cols(agg, t)
                        cols = (dinv_all[:, NODES * t:NODES * (t + 1)] if isinstance(t, int)
                                else dinv_all[:, ds(NODES * t, NODES)])
                        nc.vector.tensor_tensor(where, where, cols.unsqueeze(1).to_broadcast([P, KC, NODES]),
                                                ALU.mult).then_inc(S["hop_scaled"], 1)

                    dve.wait_ge(S["h0_agg_added"], NG)
                    dve.wait_ge(S["dinv_squared"], 1)
                    over_nodes(dve, lambda i, u: at_tile(scale_hop, i, u, 0), 0, NN)
                    dve.wait_ge(S["win_copied"], 2 * NN)

            def logit_rows(t, h):
                dve.wait_ge(S["logits_done"], t + 1)
                nc.vector.scalar_tensor_tensor(out=logit_rows_t[:, h, :], in0=banks[0:NODES, h % 2, 0:H],
                                               scalar=column(dinv_col, t), in1=bias_l[0:NODES, :], op0=ALU.mult,
                                               op1=ALU.add).then_inc(S["logit_rows"], 1)

            def logit_top(t, h):
                dve.wait_ge(S["logit_rows"], t + 1)
                nc.vector.tensor_reduce(top[:, h, 0:1], logit_rows_t[:, h, :], AX.X, ALU.max).then_inc(S["logit_top"], 1)

            def less_top(t, h):
                dve.wait_ge(S["logit_top"], t + 1)
                nc.vector.tensor_single_scalar(top[:, h, 1:2], top[:, h, 0:1], -1.0, ALU.mult).then_inc(S["l_chain"], 1)

            def add_logits(t, h):
                dve.wait_ge(S["l_chain"], t + 1)
                nc.vector.scalar_tensor_tensor(out=x3_rows(t), in0=logit_rows_t[:, h, :], scalar=top[:, h, 1:2],
                                               in1=x3_rows(t), op0=ALU.add, op1=ALU.add).then_inc(S["y_added"], 1)

            def logit_step(i, u):
                at_tile(logit_rows, i, u, 0, slots=4)
                at_tile(logit_top, i, u, -1, slots=4)
                at_tile(add_logits, i, u, -2, slots=4)
                at_tile(less_top, i, u, -1, slots=4)

            over_nodes(dve, logit_step, 0, NN + 2)

            def last_sum(t, h):
                wait_count(dve, S["y_ready"], t - 3)
                nc.vector.tensor_scalar(logit_rows_t[:, h, :], x3_rows(t), column(lse, t), None,
                                        ALU.subtract).then_inc(S["y_summed"], 1)

            def last_reciprocal(t, h):
                dve.wait_ge(S["y_deviation"], t + 1)
                nc.vector.reciprocal(last_scale[:, h:h + 1], last_scale[:, h:h + 1]).then_inc(S["y_scale"], 1)

            def last_less_mean(t, h):
                dve.wait_ge(S["y_scale"], t + 1)
                nc.vector.scalar_tensor_tensor(out=last_shift[:, h:h + 1], in0=last_moments_t[:, h, 0:1], scalar=-1.0,
                                               in1=last_scale[:, h:h + 1], op0=ALU.mult, op1=ALU.mult).then_inc(
                    S["y_shift"], 1)

            def last_statistics(t, h):
                dve.wait_ge(S["y_summed"], t + 1)
                nc.vector.bn_stats(last_stats[:, h, :], logit_rows_t[:, h, :]).then_inc(S["y_stats"], 1)

            def last_moments(t, h):
                if isinstance(t, int) and t == NN - 1:
                    dve.wait_ge(S["y_stats"], t + 1)
                    dve.sem_inc(S["begun"], 1)
                nc.vector.bn_aggr(last_moments_t[:, h, :], last_stats[:, h, :]).then_inc(S["y_moments"], 1)

            def last_step(i, u):
                at_tile(last_reciprocal, i, u, -3, slots=4)
                at_tile(last_sum, i, u, 0, slots=4)
                at_tile(last_less_mean, i, u, -3, slots=4)
                at_tile(last_statistics, i, u, 0, slots=4)
                at_tile(last_moments, i, u, -1, slots=4)

            dve.wait_ge(S["lse_ready"], 1)
            dve.wait_ge(S["y_added"], NN)
            over_nodes(dve, last_step, 0, NN + 3)


_INS = ["x", "src", "dst", "edge_attr_64", "L0_gnn_W1", "L0_gnn_b1", "L0_gnn_W2", "L0_gnn_b2", "L0_gnn_Wg",
        "L0_gnn_bg", "L0_gnn_gamma", "L0_gnn_beta", "L1_gnn_W", "L1_gnn_b"]


def kernel(**inputs):
    import concourse.bacc as bacc
    from concourse.bass_utils import run_bass_kernel_spmd

    nc = bacc.Bacc("TRN2", target_bir_lowering=False, num_devices=1)
    arrays, args = {}, []
    for name in _INS:
        a = np.ascontiguousarray(inputs[name])
        arrays[f"in_{name}"] = a
        args.append(nc.dram_tensor(f"in_{name}", a.shape, mybir.dt.from_np(a.dtype), kind="ExternalInput").ap())
    out = nc.dram_tensor("out", inputs["x"].shape, F32, kind="ExternalOutput").ap()
    gnn_kernel(nc, *args, out)
    result = run_bass_kernel_spmd(nc, [arrays], core_ids=[0])
    return result.results[0]["out"]
```
